# Optimizing a Trainium2 kernel written in Bass

```python
import numpy as np
import jax
import jax.numpy as jnp

def _softmax(x, axis=-1):
    return jax.nn.softmax(x, axis=axis)

def _gelu(x):
    return jax.nn.gelu(x, approximate=True)

def _silu(x):
    return jax.nn.silu(x)

def _sigmoid(x):
    return jax.nn.sigmoid(x)

def _layernorm(x, axis=-1, eps=1e-05):
    m = jnp.mean(x, axis=axis, keepdims=True)
    v = jnp.var(x, axis=axis, keepdims=True)
    return (x - m) / jnp.sqrt(v + eps)

def _scatter_add(tgt, idx, src, axis=0):
    return tgt.at[idx].add(src)

def _segment_sum(src, seg, n):
    return jax.ops.segment_sum(src, seg, n)
kernel_name = 'mk_vit_tower_d1_tok_img768_r4_cf57db'

def setup_inputs(seed: int=0):
    np.random.seed(seed)
    _w = jnp.asarray

    def _rec_inputs():
        import jax
        import jax.numpy as jnp
        _rk = jax.random.key(seed)
        x = -0.00016672 + 0.999947 * jax.random.normal(jax.random.fold_in(_rk, 1), (32, 96, 96, 3), jnp.float32)
        return x
    x = _rec_inputs()

    def _L0_tok_setup():
        import jax, jax.numpy as jnp
        import numpy as np
        P = 16

        def _extract_patches(images, p):
            B, H, W, C = images.shape
            gh, gw = (H // p, W // p)
            x = images.reshape(B, gh, p, gw, p, C)
            x = x.transpose(0, 1, 3, 2, 4, 5)
            return x.reshape(B, gh * gw, p * p * C)
        key = jax.random.key(seed)
        k1, k2, k3 = jax.random.split(key, 3)
        B, H, Wd, C = (64, 96, 96, 3)
        dims = 192
        patch_dim = P * P * C
        num_patches = H // P * (Wd // P)
        images = jax.random.normal(k1, (B, H, Wd, C), dtype=jnp.float32)
        W = jax.random.normal(k2, (patch_dim, dims), dtype=jnp.float32) * patch_dim ** (-0.5)
        b = jnp.zeros((dims,), dtype=jnp.float32)
        emb_table = jax.random.normal(k3, (num_patches + 2, dims), dtype=jnp.float32) * 0.02
        return {'images': images, 'W': W, 'b': b, 'emb_table': emb_table}
    _L0_tok_all = _L0_tok_setup()
    _L0_tok_in = {k: v for k, v in _L0_tok_all.items() if k in ('W', 'b', 'emb_table')}
    del _L0_tok_all

    def _L0_attn_setup():
        import jax, jax.numpy as jnp
        import numpy as np
        NUM_HEADS = 12
        NUM_LANDMARKS = 64
        PINV_ITERS = 6

        def moore_penrose_iter_pinv(x, iters=PINV_ITERS):
            abs_x = jnp.abs(x)
            col = abs_x.sum(axis=-1)
            row = abs_x.sum(axis=-2)
            z = jnp.swapaxes(x, -1, -2) / (jnp.max(col) * jnp.max(row))
            I = jnp.eye(x.shape[-1], dtype=x.dtype)
            for _ in range(iters):
                xz = x @ z
                z = 0.25 * z @ (13.0 * I - xz @ (15.0 * I - xz @ (7.0 * I - xz)))
            return z

        def _reference_tuple_inner(x, w_qkv, w_proj, b_proj):
            B, N, C = x.shape
            H = NUM_HEADS
            m = NUM_LANDMARKS
            d = C // H
            scale = d ** (-0.5)
            original_N = N
            rem = N % m
            if rem > 0:
                x = jnp.pad(x, ((0, 0), (m - rem, 0), (0, 0)))
                N = x.shape[1]
            qkv = x @ w_qkv.T
            q, k, v = jnp.split(qkv, 3, axis=-1)
            to_heads = lambda t: t.reshape(B, N, H, d).transpose(0, 2, 1, 3)
            q, k, v = (to_heads(q), to_heads(k), to_heads(v))
            q = q * scale
            l = N // m
            q_landmarks = q.reshape(B, H, m, l, d).mean(axis=3)
            k_landmarks = k.reshape(B, H, m, l, d).mean(axis=3)
            sim1 = jnp.einsum('bhnd,bhmd->bhnm', q, k_landmarks)
            sim2 = jnp.einsum('bhid,bhjd->bhij', q_landmarks, k_landmarks)
            sim3 = jnp.einsum('bhmd,bhnd->bhmn', q_landmarks, k)
            attn1 = jax.nn.softmax(sim1, axis=-1)
            attn2 = jax.nn.softmax(sim2, axis=-1)
            attn3 = jax.nn.softmax(sim3, axis=-1)
            attn2_inv = moore_penrose_iter_pinv(attn2, PINV_ITERS)
            attn = attn1 @ attn2_inv @ attn3
            out = attn1 @ (attn2_inv @ (attn3 @ v))
            out = out.transpose(0, 2, 1, 3).reshape(B, N, C)
            out = out[:, -original_N:]
            out = out @ w_proj.T + b_proj
            return (out, attn)
        key = jax.random.key(seed)
        k1, k2, k3, k4 = jax.random.split(key, 4)
        B, N, C = (2, 512, 192)
        x = jax.random.normal(k1, (B, N, C), dtype=jnp.float32)
        w_qkv = jax.random.normal(k2, (3 * C, C), dtype=jnp.float32) * 0.02
        w_proj = jax.random.normal(k3, (C, C), dtype=jnp.float32) * 0.02
        b_proj = jax.random.normal(k4, (C,), dtype=jnp.float32) * 0.02
        return {'x': x, 'w_qkv': w_qkv, 'w_proj': w_proj, 'b_proj': b_proj}
    _L0_attn_all = _L0_attn_setup()
    _L0_attn_in = {k: v for k, v in _L0_attn_all.items() if k in ('w_qkv', 'w_proj', 'b_proj')}
    del _L0_attn_all

    def _L0_ffn_setup():
        import jax, jax.numpy as jnp
        import numpy as np
        EPS = 1e-05

        def _ln(x, g, b):
            m = jnp.mean(x, axis=-1, keepdims=True)
            v = jnp.mean((x - m) ** 2, axis=-1, keepdims=True)
            return (x - m) / jnp.sqrt(v + EPS) * g + b
        key = jax.random.key(seed)
        ks = jax.random.split(key, 16)
        B, S, D, H, E, K = (32, 128, 192, 12, 8, 2)
        Dff = 4 * D
        s = 0.02
        return {'x': jax.random.normal(ks[0], (B, S, D), dtype=jnp.float32), 'ln1_g': jnp.ones((D,), jnp.float32), 'ln1_b': jnp.zeros((D,), jnp.float32), 'in_proj_w': jax.random.normal(ks[1], (3 * D, D), jnp.float32) * s, 'in_proj_b': jnp.zeros((3 * D,), jnp.float32), 'out_proj_w': jax.random.normal(ks[2], (D, D), jnp.float32) * s, 'out_proj_b': jnp.zeros((D,), jnp.float32), 'ln2_g': jnp.ones((D,), jnp.float32), 'ln2_b': jnp.zeros((D,), jnp.float32), 'router_w': jax.random.normal(ks[3], (E, D), jnp.float32) * s, 'router_b': jnp.zeros((E,), jnp.float32), 'w1': jax.random.normal(ks[4], (E, D, Dff), jnp.float32) * s, 'b1': jnp.zeros((E, Dff), jnp.float32), 'w2': jax.random.normal(ks[5], (E, Dff, D), jnp.float32) * s, 'b2': jnp.zeros((E, D), jnp.float32)}
    _L0_ffn_all = _L0_ffn_setup()
    _L0_ffn_in = {k: v for k, v in _L0_ffn_all.items() if k in ('ln1_g', 'ln1_b', 'in_proj_w', 'in_proj_b', 'out_proj_w', 'out_proj_b', 'ln2_g', 'ln2_b', 'router_w', 'router_b', 'w1', 'b1', 'w2', 'b2')}
    del _L0_ffn_all
    return {'x': x, 'L0_tok_W': _L0_tok_in['W'], 'L0_tok_b': _L0_tok_in['b'], 'L0_tok_emb_table': _L0_tok_in['emb_table'], 'L0_attn_w_qkv': _L0_attn_in['w_qkv'], 'L0_attn_w_proj': _L0_attn_in['w_proj'], 'L0_attn_b_proj': _L0_attn_in['b_proj'], 'L0_ffn_ln1_g': _L0_ffn_in['ln1_g'], 'L0_ffn_ln1_b': _L0_ffn_in['ln1_b'], 'L0_ffn_in_proj_w': _L0_ffn_in['in_proj_w'], 'L0_ffn_in_proj_b': _L0_ffn_in['in_proj_b'], 'L0_ffn_out_proj_w': _L0_ffn_in['out_proj_w'], 'L0_ffn_out_proj_b': _L0_ffn_in['out_proj_b'], 'L0_ffn_ln2_g': _L0_ffn_in['ln2_g'], 'L0_ffn_ln2_b': _L0_ffn_in['ln2_b'], 'L0_ffn_router_w': _L0_ffn_in['router_w'], 'L0_ffn_router_b': _L0_ffn_in['router_b'], 'L0_ffn_w1': _L0_ffn_in['w1'], 'L0_ffn_b1': _L0_ffn_in['b1'], 'L0_ffn_w2': _L0_ffn_in['w2'], 'L0_ffn_b2': _L0_ffn_in['b2']}

def reference(x, L0_tok_W, L0_tok_b, L0_tok_emb_table, L0_attn_w_qkv, L0_attn_w_proj, L0_attn_b_proj, L0_ffn_ln1_g, L0_ffn_ln1_b, L0_ffn_in_proj_w, L0_ffn_in_proj_b, L0_ffn_out_proj_w, L0_ffn_out_proj_b, L0_ffn_ln2_g, L0_ffn_ln2_b, L0_ffn_router_w, L0_ffn_router_b, L0_ffn_w1, L0_ffn_b1, L0_ffn_w2, L0_ffn_b2):
    import jax
    import jax.numpy as jnp

    def _L0_tok_ref(images, W, b, emb_table):
        import jax, jax.numpy as jnp
        import numpy as np
        P = 16

        def _extract_patches(images, p):
            B, H, W, C = images.shape
            gh, gw = (H // p, W // p)
            x = images.reshape(B, gh, p, gw, p, C)
            x = x.transpose(0, 1, 3, 2, 4, 5)
            return x.reshape(B, gh * gw, p * p * C)
        patches = _extract_patches(images, P)
        x = jnp.einsum('bnd,de->bne', patches, W) + b
        cls = jnp.zeros_like(x[:, :1, :])
        x = jnp.concatenate([cls, x], axis=1)
        n_tok = x.shape[1]
        pos = emb_table[:n_tok]
        return x + pos[None]

    def _L0_attn_ref(x, w_qkv, w_proj, b_proj):
        import jax, jax.numpy as jnp
        import numpy as np
        NUM_HEADS = 12
        NUM_LANDMARKS = 64
        PINV_ITERS = 6

        def moore_penrose_iter_pinv(x, iters=PINV_ITERS):
            abs_x = jnp.abs(x)
            col = abs_x.sum(axis=-1)
            row = abs_x.sum(axis=-2)
            z = jnp.swapaxes(x, -1, -2) / (jnp.max(col) * jnp.max(row))
            I = jnp.eye(x.shape[-1], dtype=x.dtype)
            for _ in range(iters):
                xz = x @ z
                z = 0.25 * z @ (13.0 * I - xz @ (15.0 * I - xz @ (7.0 * I - xz)))
            return z

        def _reference_tuple_inner(x, w_qkv, w_proj, b_proj):
            B, N, C = x.shape
            H = NUM_HEADS
            m = NUM_LANDMARKS
            d = C // H
            scale = d ** (-0.5)
            original_N = N
            rem = N % m
            if rem > 0:
                x = jnp.pad(x, ((0, 0), (m - rem, 0), (0, 0)))
                N = x.shape[1]
            qkv = x @ w_qkv.T
            q, k, v = jnp.split(qkv, 3, axis=-1)
            to_heads = lambda t: t.reshape(B, N, H, d).transpose(0, 2, 1, 3)
            q, k, v = (to_heads(q), to_heads(k), to_heads(v))
            q = q * scale
            l = N // m
            q_landmarks = q.reshape(B, H, m, l, d).mean(axis=3)
            k_landmarks = k.reshape(B, H, m, l, d).mean(axis=3)
            sim1 = jnp.einsum('bhnd,bhmd->bhnm', q, k_landmarks)
            sim2 = jnp.einsum('bhid,bhjd->bhij', q_landmarks, k_landmarks)
            sim3 = jnp.einsum('bhmd,bhnd->bhmn', q_landmarks, k)
            attn1 = jax.nn.softmax(sim1, axis=-1)
            attn2 = jax.nn.softmax(sim2, axis=-1)
            attn3 = jax.nn.softmax(sim3, axis=-1)
            attn2_inv = moore_penrose_iter_pinv(attn2, PINV_ITERS)
            attn = attn1 @ attn2_inv @ attn3
            out = attn1 @ (attn2_inv @ (attn3 @ v))
            out = out.transpose(0, 2, 1, 3).reshape(B, N, C)
            out = out[:, -original_N:]
            out = out @ w_proj.T + b_proj
            return (out, attn)
        return _reference_tuple_inner(x, w_qkv, w_proj, b_proj)[0]

    def _L0_ffn_ref(x, ln1_g, ln1_b, in_proj_w, in_proj_b, out_proj_w, out_proj_b, ln2_g, ln2_b, router_w, router_b, w1, b1, w2, b2):
        import jax, jax.numpy as jnp
        import numpy as np
        EPS = 1e-05

        def _ln(x, g, b):
            m = jnp.mean(x, axis=-1, keepdims=True)
            v = jnp.mean((x - m) ** 2, axis=-1, keepdims=True)
            return (x - m) / jnp.sqrt(v + EPS) * g + b
        B, S, D = x.shape
        H = 12
        Dh = D // H
        E = router_w.shape[0]
        K = 2
        x2 = _ln(x, ln1_g, ln1_b)
        qkv = x2 @ in_proj_w.T + in_proj_b
        q, k, v = jnp.split(qkv, 3, axis=-1)
        q = q.reshape(B, S, H, Dh)
        k = k.reshape(B, S, H, Dh)
        v = v.reshape(B, S, H, Dh)
        scores = jnp.einsum('bqhd,bkhd->bhqk', q, k) / jnp.sqrt(jnp.float32(Dh))
        attn = jax.nn.softmax(scores, axis=-1)
        ao = jnp.einsum('bhqk,bkhd->bqhd', attn, v).reshape(B, S, D)
        ao = ao @ out_proj_w.T + out_proj_b
        x = x + ao
        xm = _ln(x, ln2_g, ln2_b).reshape(B * S, D)
        T = B * S
        logits = xm @ router_w.T + router_b
        probs = jax.nn.softmax(logits, axis=-1)
        topw, topi = jax.lax.top_k(probs, K)
        topw = topw / jnp.sum(topw, axis=-1, keepdims=True)
        combine = jnp.zeros((T, E), xm.dtype).at[jnp.arange(T)[:, None], topi].add(topw)
        out = jnp.zeros_like(xm)
        for e in range(E):
            h = jax.nn.gelu(xm @ w1[e] + b1[e], approximate=False)
            y = h @ w2[e] + b2[e]
            out = out + combine[:, e:e + 1] * y
        x = x + out.reshape(B, S, D)
        return x
    h = _L0_tok_ref(x, L0_tok_W, L0_tok_b, L0_tok_emb_table)
    h = h + _L0_attn_ref(_layernorm(h, axis=-1), L0_attn_w_qkv, L0_attn_w_proj, L0_attn_b_proj)
    h = h + _L0_ffn_ref(_layernorm(h, axis=-1), L0_ffn_ln1_g, L0_ffn_ln1_b, L0_ffn_in_proj_w, L0_ffn_in_proj_b, L0_ffn_out_proj_w, L0_ffn_out_proj_b, L0_ffn_ln2_g, L0_ffn_ln2_b, L0_ffn_router_w, L0_ffn_router_b, L0_ffn_w1, L0_ffn_b1, L0_ffn_w2, L0_ffn_b2)
    return h

_drawn_inputs = setup_inputs


def setup_inputs(seed=0):
    import zlib

    import numpy as np

    out = dict(_drawn_inputs(seed))
    spreads = {'L0_tok_b': (0.0, 0.1),
     'L0_ffn_ln1_g': (1.0, 0.6),
     'L0_ffn_ln1_b': (0.0, 0.8),
     'L0_ffn_in_proj_b': (0.0, 0.491),
     'L0_ffn_out_proj_b': (0.0, 0.1),
     'L0_ffn_ln2_g': (1.0, 0.6),
     'L0_ffn_ln2_b': (0.0, 0.683),
     'L0_ffn_router_b': (0.0, 0.338),
     'L0_ffn_b1': (0.0, 0.723),
     'L0_ffn_b2': (0.0, 0.327)}
    factors = {'L0_ffn_in_proj_w': 5.293, 'L0_ffn_out_proj_w': 3.159}
    for name, (base, spread) in spreads.items():
        noise = np.random.default_rng([zlib.crc32(name.encode()), seed]).standard_normal(out[name].shape)
        drawn = base * np.exp(spread * noise) if base else spread * noise
        out[name] = jnp.asarray(drawn.astype(out[name].dtype))
    for name, factor in factors.items():
        out[name] = (out[name] * factor).astype(out[name].dtype)
    return out
```

```python
from contextlib import ExitStack

import numpy as np
import concourse.bass as bass
from concourse import mybir

F32 = mybir.dt.float32
ALU = mybir.AluOpType
ACT = mybir.ActivationFunctionType
AX = mybir.AxisListType

IMAGES, GRID, PATCH, D = 32, 6, 16, 192
TOK = GRID * GRID + 1
PADS = 64 - TOK
S = TOK + 1
NB = 3
R = NB * S
T = -(-IMAGES // NB)
FIRST_IMAGE = [min(NB * t, IMAGES - NB) for t in range(T)]
PD = PATCH * PATCH * 3
PC = PD // 128
H, DH = 12, 16
HC, CH = 4, 3
KB = D - 128
ONES = KB
AUG = KB + 7
GROUPS = T * H
BG = 11
STREAMS = 3
ROUNDS = GROUPS // (BG * STREAMS)
ITERS = 6
E, DFF = 8, 768
FC = DFF // 128
EPS = 1e-5
MASK = -(2.0 ** 40)
ROOT = float(np.float32(np.sqrt(PADS)))

C_ID, C_IC, C_MASK, C_W, C_WINV, C_HALF = 0, 128, 166, 169, 170, 171
C_COLS = 172


def build(nc, patches, pos, consts, aug1, aug2, w_tok, b_tok, row_mask, wqk1, wv1, wproj1, wqk2, wv2,
          wproj2, router, w1, b1, w2, b2, affine, out):
    with ExitStack() as ctx:
        def sb(name, shape):
            return ctx.enter_context(nc.sbuf_tensor(name, shape, F32))

        def psum(name, shape):
            return ctx.enter_context(nc.psum_tensor(name, shape, F32))

        def sem(name):
            return ctx.enter_context(nc.semaphore(name))

        def sems(name, n):
            return [sem(f"{name}{i}") for i in range(n)]

        cst = sb("cst", [128, C_COLS])
        ident = cst[:, C_ID:C_ID + 128]
        neg_eye = cst[0:R, C_IC:C_IC + S]
        in_image = cst[0:R, C_MASK:C_MASK + NB]
        wcol = cst[0:R, C_W:C_W + 1]
        winv = cst[0:R, C_WINV:C_WINV + 1]
        half = cst[0:R, C_HALF:C_HALF + 1]
        wtok = sb("wtok", [128, PC, D])
        btok = sb("btok", [1, D])
        rmask = sb("rmask", [1, R])
        post = sb("post", [R, D])
        wqk = [[sb(f"wqk{l}{k}", [128, 2, CH * 128]) for k in range(2)] for l in range(2)]
        wv = [[sb(f"wv{l}{k}", [128, D]) for k in range(2)] for l in range(2)]
        wo = [[sb(f"wo{l}{k}", [128, D]) for k in range(2)] for l in range(2)]
        wr = [sb(f"wr{k}", [128, E]) for k in range(2)]
        b2t = sb("b2t", [E, D])
        aff = sb("aff", [128, 8])
        b1t = sb("b1t", [128, E, FC])

        pt = sb("pt", [128, PC * R])
        nrm = sb("nrm", [R, D])
        stats = sb("stats", [R, 6])
        mv = sb("mv", [R, 2])
        veps = sb("veps", [R, 1])
        rstd = sb("rstd", [R, 1])
        xta = sb("xta", [128, R])
        xtb1 = sb("xtb1", [128, R])
        xtb2 = sb("xtb2", [128, R])
        qt = sb("qt", [128, CH * R])
        ktm = sb("ktm", [128, CH, HC, R])
        vw = sb("vw", [R, H, DH + 1])
        v1 = sb("v1", [R, H, DH + 1])
        mx = sb("mx", [R, CH, HC])
        zs = sb("zs", [R, CH, HC])
        zp = sb("zp", [R, CH, HC])
        zr = sb("zr", [R, CH, HC])
        sd = sb("sd", [R, CH, HC, R])
        pr = sb("pr", [R, CH, HC, R])
        prt = sb("prt", [R, CH, HC, R])
        hall = sb("hall", [R, T, D])
        uall = sb("uall", [R, T, D])
        gall = sb("gall", [R, GROUPS, S])
        avall = sb("avall", [R, GROUPS, DH + 2])
        noall = sb("noall", [R, GROUPS, DH])
        comball = sb("comball", [R, T, E])
        red = sb("red", [R, 2])
        redall = sb("redall", [R, 2])
        cc = sb("cc", [R, 1])
        cinv = sb("cinv", [R, 1])
        X = [sb(f"x_{s}", [R, BG, S]) for s in range(STREAMS)]
        PS = [sb(f"ps_{s}", [R, BG, S]) for s in range(STREAMS)]
        Y = [sb(f"y_{s}", [R, BG, S]) for s in range(STREAMS)]
        W = [sb(f"w_{s}", [R, BG, S]) for s in range(STREAMS)]
        shared = sb("shared", [128, 2 * STREAMS * BG * R])
        forms = shared[0:R, :].rearrange("p (s g n) -> p s g n", g=BG, n=R)
        BX = [forms[:, s] for s in range(STREAMS)]
        BP = [forms[:, STREAMS + s] for s in range(STREAMS)]
        nos = sb("nos", [R, D])
        aot = [sb(f"aot{k}", [128, R]) for k in range(2)]
        aos = sb("aos", [R, D])
        xps = sb("xps", [R, D])
        xmt = [sb(f"xmt{k}", [128, R]) for k in range(2)]
        xmall = [sb(f"xmall{k}", [128, T * R]) for k in range(2)]
        lg = sb("lg", [R, 2 * E])
        top8 = sb("top8", [R, 8])
        top2 = sb("top2", [R, 8])
        lrep = sb("lrep", [R, 2 * E])
        sel = sb("sel", [R, E])
        lsh = sb("lsh", [R, E])
        pe8 = sb("pe8", [R, E])
        psel = sb("psel", [R, E])
        psum1 = sb("psum1", [R, 1])
        pinv1 = sb("pinv1", [R, 1])
        cmb = sb("cmb", [R, E])
        cmbt = sb("cmbt", [E, R])
        w1t = [[sb(f"w1t{p}{k}", [128, DFF]) for k in range(2)] for p in range(2)]
        w2t = [sb(f"w2t{p}", [128, FC, D]) for p in range(2)]
        ht = [shared[:, p * FC * NB * R:(p + 1) * FC * NB * R].rearrange("p (f n) -> p f n", f=FC) for p in range(2)]

        bank = [psum(f"bank{i}", [128, 512]) for i in range(8)]
        scp, btp, gp, avp, f0, f1 = bank[0:3], bank[3], bank[4], bank[5], bank[6], bank[7]
        p_bank, q_bank, n_bank = bank[0:3], bank[3:6], f0
        h_bank, y_bank = [*bank[0:3], f1], [*bank[3:6], f0]

        consts_in = sem("consts_in")
        weights_in = sem("weights_in")
        patches_in = sem("patches_in")
        out_done = sem("out_done")
        fixed = sem("fixed")
        bias_ps = sem("bias_ps")
        post_done = sem("post_done")

        def layer_sems(l):
            names = ["lin_ps", "lin_sb", "var_done", "rstd_done", "norm_done", "xt_ps", "xt_sb",
                     "q_ps", "k_ps", "v_ps", "q_sb", "k_sb", "v_sb", "prt_ps", "prt_sb", "g_sb", "av_sb",
                     "pool_step", "dve_step"]
            d = {n: sem(f"{n}_{l}") for n in names}
            d["sc_ps"] = sems(f"sc_ps_{l}_", CH)
            d["g_ps"] = sems(f"g_ps_{l}_", CH)
            d["sub_done"] = sems(f"sub_done_{l}_", CH)
            d["exp_done"] = sems(f"exp_done_{l}_", CH)
            d["pr_done"] = sems(f"pr_done_{l}_", CH)
            return d

        L1, L2 = layer_sems(1), layer_sems(2)
        red_done = sem("red_done")
        redall_done = sem("redall_done")
        dve_step2 = sem("dve_step2")
        pool_step2 = sem("pool_step2")
        x_done = sems("x_done", STREAMS)
        y_done = sems("y_done", STREAMS)
        ps_done = sems("ps_done", STREAMS)
        w_done = sems("w_done", STREAMS)
        bx_done = sems("bx_done", STREAMS)
        bp_done = sems("bp_done", STREAMS)
        p_ps = sems("p_ps", STREAMS)
        q_ps = sems("q_ps", STREAMS)
        n_ps = sems("n_ps", STREAMS)
        n_sb = sem("n_sb")
        nos_done, not_ps, not_sb = sem("nos_done"), sem("not_ps"), sem("not_sb")
        hres_done = sem("hres_done")
        ao_done, aot_ps, aot_sb = sem("ao_done"), sem("aot_ps"), sem("aot_sb")
        mix_ps, xp_done = sem("mix_ps"), sem("xp_done")
        acc_done = sem("acc_done")
        norm2_done, xmt_ps, xmt_sb = sem("norm2_done"), sem("xmt_ps"), sem("xmt_sb")
        xmall_done = sem("xmall_done")
        router_ps, lsh_done, pe8_done = sem("router_ps"), sem("lsh_done"), sem("pe8_done")
        cmb_done, cmbt_ps, cmbt_sb = sem("cmb_done"), sem("cmbt_ps"), sem("cmbt_sb")
        b2_ps, b2_done = sem("b2_ps"), sem("b2_done")
        expert_in = sems("expert_in", 2)
        h_ps = sem("h_ps")
        gelu_done = sems("gelu_done", 4)
        y_ps = sems("y_ps", 2)
        y_used = sems("y_used", 4)

        BLOCKS = [(0, 3), (3, 3), (6, 3), (9, 2)]
        Y_USES = [len([j for j in range(T) if j % 4 == b]) for b in range(4)]
        Y_TILES = [[j for k in (b, b + 2) for j in range(BLOCKS[k][0], sum(BLOCKS[k]))] for b in range(2)]

        started = sem("started")

        primed = [ao_done, *y_done, *w_done, *n_ps, n_sb, not_ps, acc_done, xmt_sb, xmall_done, b2_done, *gelu_done, *y_ps, *y_used]
        for L in (L1, L2):
            primed += [*L["sub_done"], *L["exp_done"], *L["g_ps"], L["prt_sb"], L["g_sb"], L["av_sb"], L["v_sb"], L["k_sb"]]

        def at(semaphore, count):
            return count + 1 if any(semaphore is x for x in primed) else count

        def gate(eng):
            eng.nop(nofuse=True)

        block = ctx.enter_context(nc.Block())

        def sc_region(c):
            return scp[c][0:R, 0:HC * R].rearrange("p (j n) -> p j n", n=R)

        def av_region(n):
            return avp[0:R, 0:HC * n].rearrange("p (j n) -> p j n", n=n)

        class Chain:

            def __init__(self, eng, sem_):
                self.eng, self.sem, self.base, self.n = eng, sem_, 0, 0

            def done(self, ins):
                self.n += 1
                ins.then_inc(self.sem, 1)

            def wait(self):
                self.eng.wait_ge(self.sem, at(self.sem, self.base + self.n))

        @block.sync
        def _(sp):
            sp.dma_start(pt[:, :], patches[:, 0, :]).then_inc(patches_in, 16)
            sp.dma_start(wtok[:, :, :], w_tok).then_inc(consts_in, 16)
            sp.dma_start(cst[:, :], consts).then_inc(consts_in, 16)
            sp.dma_start(btok[:, :], b_tok).then_inc(consts_in, 16)
            sp.dma_start(rmask[:, :], row_mask).then_inc(consts_in, 16)
            sp.dma_start(post[:, :], pos).then_inc(consts_in, 16)
            sp.dma_start(xtb1[KB:AUG, :], aug1).then_inc(consts_in, 16)
            sp.dma_start(xtb2[KB:AUG, :], aug2).then_inc(consts_in, 16)
            for k, (lo, hi) in enumerate([(0, 128), (128, 128 + AUG)]):
                sp.dma_start(wqk[0][k][0:hi - lo, :, :], wqk1[lo:hi, :, :]).then_inc(consts_in, 16)
            for k, (lo, hi) in enumerate([(0, 128), (128, D)]):
                sp.dma_start(wv[0][k][0:hi - lo, :], wv1[lo:hi, :]).then_inc(consts_in, 16)
            with sp.Fori(1, T) as t:
                sp.wait_ge(L1["lin_ps"], at(L1["lin_ps"], t))
                sp.dma_start(pt[:, :], patches[:, t, :]).then_inc(patches_in, 16)
            for k, (lo, hi) in enumerate([(0, 128), (128, 128 + AUG)]):
                sp.dma_start(wqk[1][k][0:hi - lo, :, :], wqk2[lo:hi, :, :]).then_inc(weights_in, 16)
            for k, (lo, hi) in enumerate([(0, 128), (128, D + 1)]):
                for dst, src in ((wv[1], wv2), (wo[0], wproj1), (wo[1], wproj2), (wr, router)):
                    sp.dma_start(dst[k][0:hi - lo, :], src[lo:hi, :]).then_inc(weights_in, 16)
            sp.dma_start(b2t[:, :], b2).then_inc(weights_in, 16)
            sp.dma_start(aff[:, :], affine).then_inc(weights_in, 16)
            sp.dma_start(b1t[:, :, :], b1).then_inc(weights_in, 16)

            def load_expert(e, p):
                for k, (lo, hi) in enumerate([(0, 128), (128, D)]):
                    sp.dma_start(w1t[p][k][0:hi - lo, :], w1[e, lo:hi, :]).then_inc(expert_in[p], 16)
                sp.dma_start(w2t[p][:, :, :], w2[e, :, :].rearrange("p (c d) -> p c d", c=FC)).then_inc(expert_in[p], 16)

            for p in range(2):
                load_expert(p, p)
            with sp.Fori(1, E // 2) as i:
                for p in range(2):
                    for b in range(2):
                        sp.wait_ge(y_ps[b], at(y_ps[b], (2 * i + p - 1) * len(Y_TILES[b])))
                    load_expert(2 * i + p, p)
            for b in range(4):
                sp.wait_ge(y_used[b], at(y_used[b], E * Y_USES[b]))
            for b in range(NB):
                src = hall[b * S:b * S + TOK, 0:T - 1, :]
                dst = out[0:NB * (T - 1), :, :].rearrange("(t b) i d -> b i t d", b=NB)[b]
                sp.dma_start(dst, src).then_inc(out_done, 16)
            for b in range(NB * T - IMAGES, NB):
                sp.dma_start(out[FIRST_IMAGE[-1] + b, :, :], hall[b * S:b * S + TOK, T - 1, :]).then_inc(out_done, 16)
            sp.wait_ge(out_done, at(out_done, 16 * (NB + NB - (NB * T - IMAGES))))

        CONSTS_IN = 16 * 11
        WEIGHTS_IN = 16 * 13
        FIXED = 6

        @block.tensor
        def _(pe):
            mm = nc.tensor.matmul

            def tr(dst, src, n):
                return nc.tensor.transpose(dst, src, ident[0:n, 0:n])

            def to_features(src):
                tr(f1[:, 0:R], src[:, 0:128], R)
                return tr(f1[0:KB, R:2 * R], src[:, 128:D], R)

            def qkv(t, l, L, xb):
                w = wqk[l]
                pe.wait_ge(L["xt_sb"], at(L["xt_sb"], 2 * (t + 1)))
                for q, dst, name in ((0, f0, "q_ps"), (1, f1, "k_ps")):
                    for c in range(CH):
                        mm(dst[:, c * R:(c + 1) * R], w[0][:, q, c * 128:(c + 1) * 128], xta[:, :], start=True, stop=False)
                        last = mm(dst[:, c * R:(c + 1) * R], w[1][0:AUG, q, c * 128:(c + 1) * 128], xb[0:AUG, :],
                                  start=False, stop=True)
                    last.then_inc(L[name], 1)
                pe.wait_ge(L["q_sb"], at(L["q_sb"], t + 1))
                kb = KB if l == 0 else KB + 1
                mm(f0[0:R, 0:D], xta[:, :], wv[l][0][:, :], start=True, stop=False)
                mm(f0[0:R, 0:D], xb[0:kb, :], wv[l][1][0:kb, :], start=False, stop=True).then_inc(L["v_ps"], 1)

            def scores(t, c, L):
                if c == 0:
                    pe.wait_ge(L["q_sb"], at(L["q_sb"], t + 1))
                    pe.wait_ge(L["k_sb"], at(L["k_sb"], HC * (t + 1)))
                pe.wait_ge(L["sub_done"][c], at(L["sub_done"][c], t))
                mm(scp[c][0:R, 0:HC * R], qt[:, c * R:(c + 1) * R], ktm[:, c, :, :].rearrange("p j n -> p (j n)"),
                   start=True, stop=True).then_inc(L["sc_ps"][c], 1)

            def transpose_probs(t, c, L, src_sem):
                pe.wait_ge(src_sem[c], at(src_sem[c], t + 1))
                pe.wait_ge(L["prt_sb"], at(L["prt_sb"], CH * t + c))
                for j in range(HC):
                    last = tr(btp[0:R, j * R:(j + 1) * R], pr[:, c, j, :], R)
                last.then_inc(L["prt_ps"], 1)

            pe.wait_ge(consts_in, at(consts_in, CONSTS_IN))
            mm(f0[0:R, 0:D], rmask[0:1, :], btok[0:1, :], start=True, stop=True).then_inc(bias_ps, 1)

            def embed(t):
                pe.wait_ge(patches_in, at(patches_in, 16 * (t + 1)))
                pe.wait_ge(L1["v_sb"], at(L1["v_sb"], t))
                if isinstance(t, int) and t == 0:
                    pe.wait_ge(post_done, at(post_done, 1))
                for k in range(PC):
                    last = mm(f0[0:R, 0:D], pt[:, k * R:(k + 1) * R], wtok[:, k, :], start=(k == 0), stop=(k == PC - 1))
                last.then_inc(L1["lin_ps"], 1)

            def hidden_to_features(t):
                pe.wait_ge(L1["norm_done"], at(L1["norm_done"], t + 1))
                pe.wait_ge(L1["k_sb"], at(L1["k_sb"], HC * t))
                to_features(nrm).then_inc(L1["xt_ps"], 1)

            def gram(t, c):
                u = CH * t + c
                pe.wait_ge(L1["prt_sb"], at(L1["prt_sb"], u + 1))
                pe.wait_ge(L1["g_sb"], at(L1["g_sb"], u))
                pe.wait_ge(L1["av_sb"], at(L1["av_sb"], u))
                if c == 0:
                    pe.wait_ge(L1["v_sb"], at(L1["v_sb"], t + 1))
                for j in range(HC):
                    mm(gp[0:R, j * R:(j + 1) * R], prt[:, c, j, :], prt[:, c, j, :], start=True, stop=True)
                av = av_region(DH + 2)
                for j in range(HC):
                    mm(av[:, j, 0:DH + 1], prt[:, c, j, :], vw[:, c * HC + j, :], start=True, stop=True)
                    last = mm(av[:, j, DH + 1:DH + 2], pr[:, c, j, :], wcol, start=True, stop=True)
                last.then_inc(L1["g_ps"][c], 1)

            def back1(t, nxt):
                for c in range(CH):
                    scores(t, c, L1)
                if nxt is not None:
                    embed(nxt)
                transpose_probs(t, 0, L1, L1["pr_done"])
                transpose_wait = L1["pr_done"]
                gram(t, 0)
                if nxt is not None:
                    hidden_to_features(nxt)
                transpose_probs(t, 1, L1, transpose_wait)
                gram(t, 1)
                transpose_probs(t, 2, L1, transpose_wait)
                gram(t, 2)
                if nxt is not None:
                    qkv(nxt, 0, L1, xtb1)

            embed(0)
            hidden_to_features(0)
            qkv(0, 0, L1, xtb1)
            with pe.Fori(0, T - 1) as t:
                back1(t, t + 1)
            back1(T - 1, None)

            with pe.Fori(0, ROUNDS) as g:
                with pe.Fori(0, ITERS) as n:
                    for s in range(STREAMS):
                        pe.wait_ge(bx_done[s], at(bx_done[s], 3 * ((ITERS + 1) * g + n + 1)))
                        for j in range(BG):
                            last = mm(p_bank[s][0:R, j * S:(j + 1) * S], BX[s][:, j, :], X[s][:, j, :], start=True, stop=True)
                        last.then_inc(p_ps[s], 1)
                    for s in range(STREAMS):
                        pe.wait_ge(bp_done[s], at(bp_done[s], 3 * (ITERS * g + n + 1)))
                        pe.wait_ge(w_done[s], at(w_done[s], ITERS * g + n + 1))
                        for j in range(BG):
                            last = mm(q_bank[s][0:R, j * S:(j + 1) * S], BP[s][:, j, :], W[s][:, j, :], start=True, stop=True)
                        last.then_inc(q_ps[s], 1)
                for s in range(STREAMS):
                    pe.wait_ge(bx_done[s], at(bx_done[s], 3 * ((ITERS + 1) * g + ITERS + 1)))
                    pe.wait_ge(n_sb, at(n_sb, STREAMS * g + s))
                    for j in range(BG):
                        last = mm(n_bank[0:R, j * DH:(j + 1) * DH], BX[s][:, j, :],
                                  avall[:, (g * STREAMS + s) * BG + j, 0:DH], start=True, stop=True)
                    last.then_inc(n_ps[s], 1)

            pe.wait_ge(weights_in, at(weights_in, WEIGHTS_IN))

            def linear(src, w):
                mm(f0[0:R, 0:D], src[0][:, :], w[0][:, :], start=True, stop=False)
                return mm(f0[0:R, 0:D], src[1][0:KB + 1, :], w[1][0:KB + 1, :], start=False, stop=True)

            def front2(t):
                pe.wait_ge(nos_done, at(nos_done, t + 1))
                pe.wait_ge(xmt_sb, at(xmt_sb, 2 * t))
                pe.wait_ge(b2_done, at(b2_done, t))
                to_features(nos).then_inc(not_ps, 1)
                pe.wait_ge(not_sb, at(not_sb, 2 * (t + 1)))
                linear(aot, wo[0]).then_inc(L2["lin_ps"], 1)
                pe.wait_ge(L2["norm_done"], at(L2["norm_done"], t + 1))
                to_features(nrm).then_inc(L2["xt_ps"], 1)
                qkv(t, 1, L2, xtb2)

            def back2(t):
                for c in range(CH):
                    scores(t, c, L2)
                for c in range(CH):
                    transpose_probs(t, c, L2, L2["exp_done"])
                    pe.wait_ge(L2["prt_sb"], at(L2["prt_sb"], CH * t + c + 1))
                    pe.wait_ge(ao_done, at(ao_done, CH * t + c))
                    if c == 0:
                        pe.wait_ge(L2["v_sb"], at(L2["v_sb"], t + 1))
                    av = av_region(DH + 1)
                    for j in range(HC):
                        last = mm(av[:, j, :], prt[:, c, j, :], v1[:, c * HC + j, :], start=True, stop=True)
                    last.then_inc(L2["g_ps"][c], 1)

            def tail2(t):
                pe.wait_ge(ao_done, at(ao_done, CH * (t + 1)))
                to_features(aos).then_inc(aot_ps, 1)
                pe.wait_ge(aot_sb, at(aot_sb, 2 * (t + 1)))
                linear(aot, wo[1]).then_inc(mix_ps, 1)
                pe.wait_ge(norm2_done, at(norm2_done, t + 1))
                to_features(nrm).then_inc(xmt_ps, 1)
                pe.wait_ge(xmt_sb, at(xmt_sb, 2 * (t + 1)))
                mm(f0[0:R, 0:E], xmt[0][:, :], wr[0][:, :], start=True, stop=False)
                mm(f0[0:R, 0:E], xmt[1][0:KB + 1, :], wr[1][0:KB + 1, :], start=False, stop=True).then_inc(router_ps, 1)
                pe.wait_ge(cmb_done, at(cmb_done, t + 1))
                tr(f0[0:E, 0:R], cmb[:, :], R).then_inc(cmbt_ps, 1)
                pe.wait_ge(cmbt_sb, at(cmbt_sb, t + 1))
                mm(f0[0:R, 0:D], cmbt[:, :], b2t[:, :], start=True, stop=True).then_inc(b2_ps, 1)

            with pe.Fori(0, T) as t:
                front2(t)
                back2(t)
                tail2(t)

            pe.wait_ge(xmall_done, at(xmall_done, 2 * T))
            pe.wait_ge(b2_done, at(b2_done, T))

            def hidden(e, p, blk):
                t0, nt = BLOCKS[blk]
                cols = slice(t0 * R, (t0 + nt) * R)
                for f in range(FC):
                    i = blk * FC + f
                    pe.wait_ge(gelu_done[i % 4], at(gelu_done[i % 4], e * FC + i // 4))
                    dst = h_bank[i % 4][:, 0:nt * R]
                    mm(dst, w1t[p][0][:, f * 128:(f + 1) * 128], xmall[0][:, cols], start=True, stop=False)
                    mm(dst, w1t[p][1][0:KB, f * 128:(f + 1) * 128], xmall[1][0:KB, cols],
                       start=False, stop=True).then_inc(h_ps, 1)

            def down(e, p, blk):
                t0, nt = BLOCKS[blk]
                for t in range(t0, t0 + nt):
                    pe.wait_ge(y_used[t % 4], at(y_used[t % 4], e * Y_USES[t % 4] + t // 4))
                    for f in range(FC):
                        if t == t0:
                            i = blk * FC + f
                            pe.wait_ge(gelu_done[i % 4], at(gelu_done[i % 4], e * FC + i // 4 + 1))
                        last = mm(y_bank[t % 4][0:R, 0:D], ht[blk % 2][:, f, (t - t0) * R:(t - t0 + 1) * R],
                                  w2t[p][:, f, :], start=(f == 0), stop=(f == FC - 1))
                    last.then_inc(y_ps[blk % 2], 1)

            with pe.Fori(0, E // 2) as i:
                for p in range(2):
                    e = 2 * i + p
                    pe.wait_ge(expert_in[p], at(expert_in[p], 48 * (i + 1)))
                    hidden(e, p, 0)
                    hidden(e, p, 1)
                    down(e, p, 0)
                    hidden(e, p, 2)
                    down(e, p, 1)
                    hidden(e, p, 3)
                    down(e, p, 2)
                    down(e, p, 3)

        @block.scalar
        def _(act):
            def copy(dst, src):
                return nc.scalar.activation(dst, src, ACT.Copy)

            def affine_out(dst, src, k, which):
                n = 128 if k == 0 else KB
                c = 4 * k + 2 * which
                return nc.scalar.activation(dst, src, ACT.Identity, bias=aff[0:n, c + 1:c + 2], scale=aff[0:n, c:c + 1])

            def q_out(t, L):
                act.wait_ge(L["q_ps"], at(L["q_ps"], t + 1))
                copy(qt[:, :], f0[:, 0:CH * R]).then_inc(L["q_sb"], 1)
                act.wait_ge(L["k_ps"], at(L["k_ps"], t + 1))
                act.wait_ge(fixed, at(fixed, FIXED))
                for j in range(0, 2):
                    q = slice(32 * j, 32 * j + 32)
                    copy(ktm[q, :, j, :], f1[q, 0:CH * R].rearrange("p (c n) -> p c n", n=R)).then_inc(L["k_sb"], 1)

            def exps(t, c, L):
                act.wait_ge(L["sub_done"][c], at(L["sub_done"][c], t + 1))
                act.wait_ge(L["g_ps"][c], at(L["g_ps"][c], t))
                nc.scalar.activation(pr[:, c], sd[:, c], ACT.Exp, scale=DH ** -0.5).then_inc(L["exp_done"][c], 1)

            def prt_out(t, c, L):
                act.wait_ge(L["prt_ps"], at(L["prt_ps"], CH * t + c + 1))
                copy(prt[:, c], btp[0:R, 0:HC * R].rearrange("p (j n) -> p j n", n=R)).then_inc(L["prt_sb"], 1)

            def front1(t):
                act.wait_ge(L1["xt_ps"], at(L1["xt_ps"], t + 1))
                copy(xta[:, :], f1[:, 0:R]).then_inc(L1["xt_sb"], 1)
                copy(xtb1[0:KB, :], f1[0:KB, R:2 * R]).then_inc(L1["xt_sb"], 1)
                q_out(t, L1)
                act.wait_ge(L1["v_ps"], at(L1["v_ps"], t + 1))
                act.wait_ge(fixed, at(fixed, FIXED))
                copy(vw[:, :, 0:DH], f0[0:R, 0:D].rearrange("p (h d) -> p h d", d=DH)).then_inc(L1["v_sb"], 1)

            def av_out(t, c):
                act.wait_ge(L1["g_ps"][c], at(L1["g_ps"][c], t + 1))
                gate(act)
                copy(avall[:, bass.ds(t * H + c * HC, HC), :], av_region(DH + 2)).then_inc(L1["av_sb"], 1)

            def back1(t, nxt):
                for c in range(CH):
                    exps(t, c, L1)
                for c in range(CH):
                    prt_out(t, c, L1)
                    av_out(t, c)
                    if c == 0 and nxt is not None:
                        act.wait_ge(L1["xt_ps"], at(L1["xt_ps"], nxt + 1))
                        copy(xta[:, :], f1[:, 0:R]).then_inc(L1["xt_sb"], 1)
                        copy(xtb1[0:KB, :], f1[0:KB, R:2 * R]).then_inc(L1["xt_sb"], 1)
                if nxt is not None:
                    q_out(nxt, L1)
                    act.wait_ge(L1["v_ps"], at(L1["v_ps"], nxt + 1))
                    copy(vw[:, :, 0:DH], f0[0:R, 0:D].rearrange("p (h d) -> p h d", d=DH)).then_inc(L1["v_sb"], 1)

            front1(0)
            with act.Fori(0, T - 1) as t:
                back1(t, t + 1)
            back1(T - 1, None)

            def spread(dst, src, done, blocks):
                for b in blocks:
                    nc.scalar.activation(dst[:, :, b * S:(b + 1) * S], src, ACT.Copy,
                                         scale=in_image[:, b:b + 1]).then_inc(done, 1)

            def groups(ap):
                return ap[:, 0:BG * S].rearrange("p (g n) -> p g n", n=S)

            with act.Fori(0, ROUNDS) as g:
                for s in range(STREAMS):
                    act.wait_ge(x_done[s], at(x_done[s], (ITERS + 1) * g + 1))
                    act.wait_ge(n_ps[s], at(n_ps[s], g))
                    spread(BX[s], X[s][:, :, :], bx_done[s], (0, 1))
                with act.Fori(0, ITERS) as n:
                    for s in range(STREAMS):
                        act.wait_ge(p_ps[s], at(p_ps[s], ITERS * g + n + 1))
                        copy(PS[s][:, :, :], groups(p_bank[s][0:R, :])).then_inc(ps_done[s], 1)
                        act.wait_ge(ps_done[s], at(ps_done[s], ITERS * g + n + 1))
                        spread(BP[s], PS[s][:, :, :], bp_done[s], (0,))
                    for s in range(STREAMS):
                        act.wait_ge(x_done[s], at(x_done[s], (ITERS + 1) * g + n + 2))
                        spread(BX[s], X[s][:, :, :], bx_done[s], (0, 1))
                for s in range(STREAMS):
                    act.wait_ge(n_ps[s], at(n_ps[s], g + 1))
                    k = (g * STREAMS + s) * BG
                    gate(act)
                    copy(noall[:, bass.ds(k, BG), :], n_bank[0:R, 0:BG * DH].rearrange("p (g n) -> p g n", n=DH)).then_inc(n_sb, 1)

            act.wait_ge(weights_in, at(weights_in, WEIGHTS_IN))
            act.wait_ge(fixed, at(fixed, FIXED))

            def out_features(dst, ready, count, done):
                act.wait_ge(ready, at(ready, count))
                copy(dst[0][:, :], f1[:, 0:R]).then_inc(done, 1)
                copy(dst[1][0:KB, :], f1[0:KB, R:2 * R]).then_inc(done, 1)

            def out_affine(dst, ready, count, done, which):
                act.wait_ge(ready, at(ready, count))
                affine_out(dst[0][:, :], f1[:, 0:R], 0, which).then_inc(done, 1)
                affine_out(dst[1][0:KB, :], f1[0:KB, R:2 * R], 1, which).then_inc(done, 1)

            with act.Fori(0, T) as t:
                out_features(aot, not_ps, t + 1, not_sb)
                out_affine([xta, xtb2], L2["xt_ps"], t + 1, L2["xt_sb"], 0)
                q_out(t, L2)
                act.wait_ge(L2["v_ps"], at(L2["v_ps"], t + 1))
                copy(v1[:, :, 0:DH], f0[0:R, 0:D].rearrange("p (h d) -> p h d", d=DH)).then_inc(L2["v_sb"], 1)
                for c in range(CH):
                    exps(t, c, L2)
                for c in range(CH):
                    prt_out(t, c, L2)
                out_features(aot, aot_ps, t + 1, aot_sb)
                act.wait_ge(xmall_done, at(xmall_done, 2 * t))
                out_affine(xmt, xmt_ps, t + 1, xmt_sb, 1)
                act.wait_ge(lsh_done, at(lsh_done, t + 1))
                nc.scalar.activation(pe8[:, :], lsh[:, :], ACT.Exp).then_inc(pe8_done, 1)
                act.wait_ge(cmbt_ps, at(cmbt_ps, t + 1))
                copy(cmbt[:, :], f0[0:E, 0:R]).then_inc(cmbt_sb, 1)

            def gelus(e, blk):
                nt = BLOCKS[blk][1]
                for f in range(FC):
                    i = blk * FC + f
                    act.wait_ge(h_ps, at(h_ps, e * FC * 4 + i + 1))
                    if f == 0:
                        act.wait_ge(y_ps[blk % 2], at(y_ps[blk % 2], e * len(Y_TILES[blk % 2]) + (3 if blk > 1 else 0)))
                    gate(act)
                    nc.scalar.activation(ht[blk % 2][:, f, 0:nt * R], h_bank[i % 4][:, 0:nt * R], ACT.Gelu,
                                         bias=b1t[:, e, f:f + 1]).then_inc(gelu_done[i % 4], 1)

            with act.Fori(0, E // 2) as i:
                for p in range(2):
                    for blk in range(4):
                        gelus(2 * i + p, blk)

        @block.vector
        def _(dve):
            V = nc.vector

            def add_norm_stats(ch, L, t, src, var_sem):
                ch.wait()
                gate(dve)
                ch.done(V.bn_stats(stats[:, :], src))
                ch.wait()
                gate(dve)
                V.bn_aggr(mv[:, :], stats[:, :]).then_inc(var_sem, 1)

            def wide(ap):
                return ap.unsqueeze(2).to_broadcast([R, HC, R])

            def softmax_shift(ch, t, c, L):
                dve.wait_ge(L["sc_ps"][c], at(L["sc_ps"][c], t + 1))
                ch.done(V.tensor_reduce(mx[:, c, :], sc_region(c), axis=AX.X, op=ALU.max))
                ch.wait()
                dve.wait_ge(L["exp_done"][c], at(L["exp_done"][c], t))
                V.tensor_tensor(sd[:, c], sc_region(c), wide(mx[:, c, :]), ALU.subtract).then_inc(L["sub_done"][c], 1)

            dve.wait_ge(consts_in, at(consts_in, CONSTS_IN))
            V.memset(ktm[:, :, :, :], 0.0).then_inc(fixed, 1)
            V.tensor_copy(vw[:, :, DH:DH + 1], wcol.unsqueeze(1).to_broadcast([R, H, 1])).then_inc(fixed, 1)
            V.memset(v1[:, :, DH:DH + 1], 1.0).then_inc(fixed, 1)
            V.memset(aot[1][KB:KB + 1, :], 1.0).then_inc(fixed, 1)
            V.memset(xmt[1][KB:KB + 1, :], 1.0).then_inc(fixed, 1)
            V.memset(lg[:, E:2 * E], -3.0e38).then_inc(fixed, 1)
            dve.wait_ge(fixed, at(fixed, FIXED))
            dve.wait_ge(bias_ps, at(bias_ps, 1))
            V.tensor_tensor(post[:, :], post[:, :], f0[0:R, 0:D], ALU.add).then_inc(post_done, 1)
            dve.wait_ge(post_done, at(post_done, 1))

            c1 = Chain(dve, L1["dve_step"])

            def front1_a(t):
                dve.wait_ge(L1["lin_ps"], at(L1["lin_ps"], t + 1))
                c1.done(V.tensor_tensor(hall[:, t, :], f0[0:R, 0:D], post[:, :], ALU.add))
                add_norm_stats(c1, L1, t, hall[:, t, :], L1["var_done"])

            def front1_b(t):
                dve.wait_ge(L1["rstd_done"], at(L1["rstd_done"], t + 1))
                V.tensor_scalar(nrm[:, :], hall[:, t, :], mv[:, 0:1], rstd[:, :], ALU.subtract, ALU.mult)\
                    .then_inc(L1["norm_done"], 1)

            def k_out(t, L):
                dve.wait_ge(L["k_ps"], at(L["k_ps"], t + 1))
                for j in range(2, HC):
                    q = slice(32 * j, 32 * j + 32)
                    V.tensor_copy(ktm[q, :, j, :], f1[q, 0:CH * R].rearrange("p (c n) -> p c n", n=R)).then_inc(L["k_sb"], 1)

            def softmax_norm(t, c):
                dve.wait_ge(L1["exp_done"][c], at(L1["exp_done"][c], t + 1))
                pads = pr[:, c].rearrange("p j (b n) -> p j b n", n=S)[:, :, :, S - 1]
                c1.done(V.tensor_reduce(zs[:, c, :], pr[:, c], axis=AX.X, op=ALU.add))
                c1.done(V.tensor_reduce(zp[:, c, :], pads, axis=AX.X, op=ALU.add))
                c1.wait()
                c1.done(V.scalar_tensor_tensor(zr[:, c, :], zp[:, c, :], float(PADS - 1), zs[:, c, :], ALU.mult, ALU.add))
                c1.wait()
                c1.done(V.reciprocal(zs[:, c, :], zr[:, c, :]))
                c1.wait()
                c1.done(V.tensor_scalar(zr[:, c, :], zs[:, c, :], wcol, None, ALU.mult))
                c1.wait()
                c1.done(V.tensor_tensor(pr[:, c], pr[:, c], wide(zr[:, c, :]), ALU.mult))
                c1.wait()
                V.tensor_scalar(pads, pads, ROOT, None, ALU.mult).then_inc(L1["pr_done"][c], 1)

            def gram_out(t, c):
                dve.wait_ge(L1["g_ps"][c], at(L1["g_ps"][c], t + 1))
                src = gp[0:R, 0:HC * R].rearrange("p (j b n) -> p j n b", j=HC, b=NB)
                V.tensor_reduce(gall[:, bass.ds(t * H + c * HC, HC), :], src, axis=AX.X, op=ALU.add)\
                    .then_inc(L1["g_sb"], 1)

            front1_a(0)
            front1_b(0)
            k_out(0, L1)
            PER = c1.n + CH * (1 + 6)
            BASE = c1.n

            def iteration(t, nxt):
                c1.base, c1.n = t * PER + BASE, 0
                for c in range(CH):
                    softmax_shift(c1, t, c, L1)
                softmax_norm(t, 0)
                if nxt is not None:
                    front1_a(nxt)
                softmax_norm(t, 1)
                gram_out(t, 0)
                if nxt is not None:
                    front1_b(nxt)
                softmax_norm(t, 2)
                gram_out(t, 1)
                gram_out(t, 2)
                if nxt is not None:
                    k_out(nxt, L1)
                    assert c1.n == PER

            with dve.Fori(0, T - 1) as t:
                iteration(t, t + 1)
            iteration(T - 1, None)

            dve.wait_ge(L1["av_sb"], at(L1["av_sb"], CH * T))
            c2 = Chain(dve, dve_step2)
            c2.done(V.tensor_reduce(red[:, :], avall[:, :, DH:DH + 2].rearrange("p g n -> p n g"), axis=AX.X, op=ALU.max))
            c2.wait()
            V.tensor_scalar(red[:, :], red[:, :], winv, None, ALU.mult).then_inc(red_done, 1)
            dve.wait_ge(redall_done, at(redall_done, 1))
            c2.done(V.tensor_tensor(cc[:, :], redall[:, 0:1], redall[:, 1:2], ALU.mult))
            c2.wait()
            c2.done(V.reciprocal(cinv[:, :], cc[:, :]))
            c2.wait()
            dve.wait_ge(L1["g_sb"], at(L1["g_sb"], CH * T))

            def spread2(dst, src, done, blocks):
                for b in blocks:
                    V.tensor_scalar(dst[:, :, b * S:(b + 1) * S], src, in_image[:, b:b + 1], None, ALU.mult).then_inc(done, 1)

            def groups(ap):
                return ap[:, 0:BG * S].rearrange("p (g n) -> p g n", n=S)

            with dve.Fori(0, ROUNDS) as g:
                for s in range(STREAMS):
                    k = (g * STREAMS + s) * BG
                    dve.wait_ge(n_ps[s], at(n_ps[s], g))
                    dve.wait_ge(y_done[s], at(y_done[s], (ITERS + 1) * g))
                    V.tensor_scalar(X[s][:, :, :], gall[:, bass.ds(k, BG), :], cinv[:, :], None, ALU.mult).then_inc(x_done[s], 1)
                    dve.wait_ge(x_done[s], at(x_done[s], (ITERS + 1) * g + 1))
                    spread2(BX[s], X[s][:, :, :], bx_done[s], (2,))
                with dve.Fori(0, ITERS) as n:
                    for s in range(STREAMS):
                        dve.wait_ge(ps_done[s], at(ps_done[s], ITERS * g + n + 1))
                        dve.wait_ge(y_done[s], at(y_done[s], (ITERS + 1) * g + n + 1))
                        V.scalar_tensor_tensor(W[s][:, :, :], PS[s][:, :, :], -0.25, Y[s][:, :, :], ALU.mult, ALU.add)\
                            .then_inc(w_done[s], 1)
                        spread2(BP[s], PS[s][:, :, :], bp_done[s], (1, 2))
                    for s in range(STREAMS):
                        dve.wait_ge(q_ps[s], at(q_ps[s], ITERS * g + n + 1))
                        V.scalar_tensor_tensor(X[s][:, :, :], X[s][:, :, :], 3.25, groups(q_bank[s][0:R, :]), ALU.mult, ALU.add)\
                            .then_inc(x_done[s], 1)
                        dve.wait_ge(x_done[s], at(x_done[s], (ITERS + 1) * g + n + 2))
                        spread2(BX[s], X[s][:, :, :], bx_done[s], (2,))

            c3 = Chain(dve, L2["dve_step"])

            def norm(c, src, var_sem, rstd_sem, count, dst):
                c.wait()
                gate(dve)
                c.done(V.bn_stats(stats[:, :], src))
                c.wait()
                gate(dve)
                V.bn_aggr(mv[:, :], stats[:, :]).then_inc(var_sem, 1)
                dve.wait_ge(rstd_sem, at(rstd_sem, count))
                return V.tensor_scalar(dst, src, mv[:, 0:1], rstd[:, :], ALU.subtract, ALU.mult)

            def tile2(t, per):
                c3.base, c3.n = t * per, 0
                var, rs = L2["var_done"], L2["rstd_done"]
                dve.wait_ge(L2["lin_ps"], at(L2["lin_ps"], t + 1))
                dve.wait_ge(acc_done, at(acc_done, t))
                c3.done(V.tensor_tensor(hall[:, t, :], hall[:, t, :], f0[0:R, 0:D], ALU.add))
                c3.done(norm(c3, hall[:, t, :], var, rs, 3 * t + 1, uall[:, t, :]))
                norm(c3, uall[:, t, :], var, rs, 3 * t + 2, nrm[:, :]).then_inc(L2["norm_done"], 1)
                k_out(t, L2)
                for c in range(CH):
                    softmax_shift(c3, t, c, L2)
                for c in range(CH):
                    dve.wait_ge(L2["g_ps"][c], at(L2["g_ps"][c], t + 1))
                    av = av_region(DH + 1)
                    c3.done(V.reciprocal(zs[:, c, :].unsqueeze(2), av[:, :, DH:DH + 1]))
                    c3.wait()
                    V.tensor_tensor(aos[:, c * HC * DH:(c + 1) * HC * DH].rearrange("p (j d) -> p j d", d=DH),
                                    av[:, :, 0:DH], zs[:, c, :].unsqueeze(2).to_broadcast([R, HC, DH]), ALU.mult)\
                        .then_inc(ao_done, 1)
                dve.wait_ge(mix_ps, at(mix_ps, t + 1))
                V.tensor_tensor(xps[:, :], uall[:, t, :], f0[0:R, 0:D], ALU.add).then_inc(xp_done, 1)
                dve.wait_ge(xp_done, at(xp_done, t + 1))
                norm(c3, xps[:, :], var, rs, 3 * t + 3, nrm[:, :]).then_inc(norm2_done, 1)
                dve.wait_ge(router_ps, at(router_ps, t + 1))
                c3.done(V.tensor_copy(lg[:, 0:E], f0[0:R, 0:E]))
                c3.wait()
                gate(dve)
                c3.done(V.max(top8[:, :], lg[:, 0:E]))
                c3.wait()
                V.tensor_scalar(lsh[:, :], lg[:, 0:E], top8[:, 0:1], None, ALU.subtract).then_inc(lsh_done, 1)
                c3.done(V.tensor_copy(top2[:, 0:2], top8[:, 0:2]))
                c3.done(V.tensor_copy(top2[:, 2:8], lg[:, E:E + 6]))
                c3.wait()
                gate(dve)
                c3.done(V.match_replace(lrep[:, :], top2[:, :], lg[:, :], 3.0e38))
                c3.wait()
                c3.done(V.tensor_tensor(sel[:, :], lrep[:, 0:E], lg[:, 0:E], ALU.not_equal))
                c3.wait()
                dve.wait_ge(pe8_done, at(pe8_done, t + 1))
                c3.done(V.tensor_tensor(psel[:, :], pe8[:, :], sel[:, :], ALU.mult))
                c3.wait()
                c3.done(V.tensor_reduce(psum1[:, :], psel[:, :], axis=AX.X, op=ALU.add))
                c3.wait()
                c3.done(V.reciprocal(pinv1[:, :], psum1[:, :]))
                c3.wait()
                V.tensor_scalar(cmb[:, :], psel[:, :], pinv1[:, :], None, ALU.mult).then_inc(cmb_done, 1)
                dve.wait_ge(cmb_done, at(cmb_done, t + 1))
                V.tensor_copy(comball[:, t, :], cmb[:, :])
                dve.wait_ge(b2_ps, at(b2_ps, t + 1))
                dve.wait_ge(acc_done, at(acc_done, t + 1))
                V.tensor_tensor(hall[:, t, :], hall[:, t, :], f0[0:R, 0:D], ALU.add).then_inc(b2_done, 1)
                return c3.n

            TILE2_STEPS = 2 + 2 + CH + CH + 1 + 8 + 1
            with dve.Fori(0, T) as t:
                n = tile2(t, TILE2_STEPS)
                assert n == TILE2_STEPS, n

            dve.wait_ge(b2_done, at(b2_done, T))
            with dve.Fori(0, E // 2) as i:
                for p in range(2):
                    e = 2 * i + p
                    for b in range(4):
                        dve.wait_ge(y_used[b], at(y_used[b], e * Y_USES[b]))
                    for j in range(T):
                        b = 0 if j in Y_TILES[0] else 1
                        dve.wait_ge(y_ps[b], at(y_ps[b], e * len(Y_TILES[b]) + Y_TILES[b].index(j) + 1))
                        V.scalar_tensor_tensor(hall[:, j, :], y_bank[j % 4][0:R, 0:D], comball[:, j, bass.ds(e, 1)], hall[:, j, :],
                                               ALU.mult, ALU.add).then_inc(y_used[j % 4], 1)

        @block.gpsimd
        def _(pool):
            G = nc.gpsimd
            for x in primed:
                pool.sem_inc(x, 1)
            pool.sem_inc(started, 1)
            pool.wait_ge(consts_in, at(consts_in, CONSTS_IN))

            def inv_sqrt(var_sem, count, step, n, done):
                pool.wait_ge(var_sem, at(var_sem, count))
                gate(pool)
                G.tensor_scalar(veps[:, :], mv[:, 1:2], EPS, None, ALU.add).then_inc(step, 1)
                pool.wait_ge(step, at(step, n))
                G.tensor_tensor(rstd[:, :], veps[:, :], half, ALU.pow).then_inc(done, 1)

            with pool.Fori(0, T) as t:
                inv_sqrt(L1["var_done"], t + 1, L1["pool_step"], t + 1, L1["rstd_done"])

            pool.wait_ge(red_done, at(red_done, 1))
            G.partition_all_reduce(redall[:, :], red[:, :], R, bass.bass_isa.ReduceOp.max).then_inc(redall_done, 1)

            eye = neg_eye.unsqueeze(1).to_broadcast([R, BG, S])

            def make_y(s, x_count, w_count, y_count):
                pool.wait_ge(x_done[s], at(x_done[s], x_count))
                pool.wait_ge(w_done[s], at(w_done[s], w_count))
                gate(pool)
                G.tensor_scalar(Y[s][:, :, :], X[s][:, :, :], 1.75, None, ALU.mult).then_inc(pool_step2, 1)
                pool.wait_ge(pool_step2, at(pool_step2, y_count))
                G.tensor_tensor(Y[s][:, :, :], Y[s][:, :, :], eye, ALU.add).then_inc(y_done[s], 1)

            with pool.Fori(0, ROUNDS) as g:
                for s in range(STREAMS):
                    make_y(s, (ITERS + 1) * g + 1, ITERS * g, STREAMS * (ITERS + 1) * g + s + 1)
                with pool.Fori(0, ITERS) as n:
                    for s in range(STREAMS):
                        make_y(s, (ITERS + 1) * g + n + 2, ITERS * g + n + 1,
                               STREAMS * ((ITERS + 1) * g + n + 1) + s + 1)

            pool.wait_ge(n_sb, at(n_sb, STREAMS * ROUNDS))
            pool.wait_ge(fixed, at(fixed, FIXED))
            with pool.Fori(0, T) as t:
                pool.wait_ge(not_ps, at(not_ps, t))
                G.tensor_copy(nos[:, :].rearrange("p (h d) -> p h d", d=DH), noall[:, bass.ds(t * H, H), :]).then_inc(nos_done, 1)
                for n in range(3):
                    inv_sqrt(L2["var_done"], 3 * t + n + 1, L2["pool_step"], 3 * t + n + 1, L2["rstd_done"])
                pool.wait_ge(xp_done, at(xp_done, t + 1))
                G.tensor_tensor(hall[:, t, :], hall[:, t, :], xps[:, :], ALU.add).then_inc(acc_done, 1)
                pool.wait_ge(xmt_sb, at(xmt_sb, 2 * (t + 1)))
                for k in range(2):
                    G.tensor_copy(xmall[k][0:[128, KB][k], bass.ds(t * R, R)], xmt[k][0:[128, KB][k], :]).then_inc(xmall_done, 1)


def kernel(**inputs):
    import concourse.bacc as bacc
    from concourse.bass_utils import run_bass_kernel_spmd

    a = {k: np.asarray(v) for k, v in inputs.items()}
    f = np.float32

    x = a["x"].reshape(IMAGES, GRID, PATCH, GRID, PATCH, 3).transpose(0, 1, 3, 2, 4, 5).reshape(IMAGES, GRID * GRID, PD)
    rows = np.zeros((T, NB, S, PD), f)
    for t in range(T):
        rows[t, :, 1:TOK] = x[FIRST_IMAGE[t]:FIRST_IMAGE[t] + NB]
    patches = rows.reshape(T, R, PC, 128).transpose(3, 0, 2, 1).reshape(128, T, PC * R)
    pos = np.zeros((NB, S, D), f)
    pos[:, 0:TOK] = a["L0_tok_emb_table"][0:TOK]
    w_tok = a["L0_tok_W"].reshape(PC, 128, D).transpose(1, 0, 2)

    consts = np.zeros((128, C_COLS), f)
    consts[:, C_ID:C_ID + 128] = np.eye(128, dtype=f)
    row_mask = np.zeros((1, NB, S), f)
    row_mask[:, :, 1:TOK] = 1
    aug = np.zeros((2, 7, NB, S), f)
    aug[:, 0] = 1
    for b in range(NB):
        consts[b * S:(b + 1) * S, C_IC:C_IC + S] = -3.75 * np.eye(S, dtype=f)
        consts[b * S:(b + 1) * S, C_MASK + b] = 1
        aug[:, 1 + b, b] = 1
        aug[:, 4 + b] = MASK
        aug[:, 4 + b, b] = 0
    aug[1, 4:7, :, S - 1] = MASK
    consts[:, C_W] = consts[:, C_WINV] = 1
    consts[S - 1:R:S, C_W] = ROOT
    consts[S - 1:R:S, C_WINV] = 1 / ROOT
    consts[:, C_HALF] = -0.5

    def qk_layout(w, bias):
        o = np.zeros((128 + AUG, 2, H, 32), f)
        for q in range(2):
            o[0:D, q, :, 0:DH] = w[q * D:(q + 1) * D].T.reshape(D, H, DH)
            if bias is not None:
                o[D, q, :, 0:DH] = bias[q * D:(q + 1) * D].reshape(H, DH)
            for b in range(NB):
                o[D + 1 + NB * q + b, q, :, DH + b] = 1
        return o.reshape(128 + AUG, 2, H * 32)

    def with_bias(w, bias):
        o = np.zeros((w.shape[1] + 1, w.shape[0]), f)
        o[:-1] = w.T
        o[-1] = bias
        return o

    wq, wi = a["L0_attn_w_qkv"], a["L0_ffn_in_proj_w"]
    bi = a["L0_ffn_in_proj_b"]
    affine = np.zeros((128, 8), f)
    for n, name in enumerate(("ln1_g", "ln1_b", "ln2_g", "ln2_b")):
        v = a["L0_ffn_" + name]
        affine[:, n] = v[0:128]
        affine[0:KB, 4 + n] = v[128:D]
    arrays = {
        "patches": patches, "pos": pos.reshape(R, D), "consts": consts,
        "aug1": aug[0].reshape(7, R), "aug2": aug[1].reshape(7, R),
        "w_tok": w_tok, "b_tok": a["L0_tok_b"].reshape(1, D), "row_mask": row_mask.reshape(1, R),
        "wqk1": qk_layout(wq, None), "wv1": wq[2 * D:].T, "wproj1": with_bias(a["L0_attn_w_proj"], a["L0_attn_b_proj"]),
        "wqk2": qk_layout(wi, bi), "wv2": with_bias(wi[2 * D:], bi[2 * D:]),
        "wproj2": with_bias(a["L0_ffn_out_proj_w"], a["L0_ffn_out_proj_b"]),
        "router": with_bias(a["L0_ffn_router_w"], a["L0_ffn_router_b"]),
        "w1": a["L0_ffn_w1"], "b1": a["L0_ffn_b1"].reshape(E, FC, 128).transpose(2, 0, 1),
        "w2": a["L0_ffn_w2"].reshape(E, FC, 128, D).transpose(0, 2, 1, 3).reshape(E, 128, FC * D),
        "b2": a["L0_ffn_b2"], "affine": affine,
    }
    arrays = {k: np.ascontiguousarray(v) for k, v in arrays.items()}
    nc = bacc.Bacc("TRN2", target_bir_lowering=False, num_devices=1)
    aps = {k: nc.dram_tensor(k, v.shape, F32, kind="ExternalInput").ap() for k, v in arrays.items()}
    out = nc.dram_tensor("out", (IMAGES, TOK, D), F32, kind="ExternalOutput").ap()
    build(nc, out=out, **aps)
    r = run_bass_kernel_spmd(nc, [arrays], core_ids=[0])
    return r.results[0]["out"]
```

```python
from contextlib import ExitStack

import numpy as np
import concourse.bass as bass
from concourse import mybir

F32 = mybir.dt.float32
ALU = mybir.AluOpType
ACT = mybir.ActivationFunctionType
AX = mybir.AxisListType

IMAGES, GRID, PATCH, D = 32, 6, 16, 192
TOK = GRID * GRID + 1
PADS = 64 - TOK
S = TOK + 1
NB = 3
R = NB * S
T = -(-IMAGES // NB)
FIRST_IMAGE = [min(NB * t, IMAGES - NB) for t in range(T)]
PD = PATCH * PATCH * 3
PC = PD // 128
H, DH = 12, 16
HC, CH = 4, 3
KB = D - 128
ONES = KB
AUG = KB + 7
GROUPS = T * H
ITERS = 6
SLOTS = 2 * ITERS
E, DFF = 8, 768
FC = DFF // 128
EPS = 1e-5
MASK = -(2.0 ** 40)
ROOT = float(np.float32(np.sqrt(PADS)))

C_ID, C_IDW, C_NEG, C_W, C_WINV, C_HALF = 0, 128, 243, 357, 358, 359
C_COLS = 360


def build(nc, patches, pos, consts, aug1, aug2, w_tok, b_tok, row_mask, wqk1, wv1, wproj1, wqk2, wv2,
          wproj2, router, w1, b1, w2, b2, affine, out):
    with ExitStack() as ctx:
        def sb(name, shape):
            return ctx.enter_context(nc.sbuf_tensor(name, shape, F32))

        def psum(name, shape):
            return ctx.enter_context(nc.psum_tensor(name, shape, F32))

        def sem(name):
            return ctx.enter_context(nc.semaphore(name))

        def sems(name, n):
            return [sem(f"{name}{i}") for i in range(n)]

        cst = sb("cst", [128, C_COLS])
        ident = cst[:, C_ID:C_ID + 128]
        idw = cst[0:R, C_IDW:C_IDW + R + 1]
        neg_eye = cst[0:R, C_NEG:C_NEG + R]
        wcol = cst[0:R, C_W:C_W + 1]
        winv = cst[0:R, C_WINV:C_WINV + 1]
        half = cst[0:R, C_HALF:C_HALF + 1]
        wtok = sb("wtok", [128, PC, D])
        btok = sb("btok", [1, D])
        rmask = sb("rmask", [1, R])
        post = sb("post", [R, D])
        wqk = [[sb(f"wqk{l}{k}", [128, 2, CH * 128]) for k in range(2)] for l in range(2)]
        wv = [[sb(f"wv{l}{k}", [128, D]) for k in range(2)] for l in range(2)]
        wo = [[sb(f"wo{l}{k}", [128, D]) for k in range(2)] for l in range(2)]
        wr = [sb(f"wr{k}", [128, E]) for k in range(2)]
        b2t = sb("b2t", [E, D])
        aff = sb("aff", [128, 8])
        b1t = sb("b1t", [128, E, FC])

        pt = sb("pt", [128, PC * R])
        nrm = sb("nrm", [R, D])
        stats = sb("stats", [R, 6])
        mv = sb("mv", [R, 2])
        veps = sb("veps", [R, 1])
        rstd = sb("rstd", [R, 1])
        xta = sb("xta", [128, R])
        xtb1 = sb("xtb1", [128, R])
        xtb2 = sb("xtb2", [128, R])
        qt = sb("qt", [128, CH * R])
        ktm = sb("ktm", [128, CH, HC, R])
        v1 = sb("v1", [R, H, DH + 1])
        mx = sb("mx", [R, CH, HC])
        zs = sb("zs", [R, CH, HC])
        zp = sb("zp", [R, CH, HC])
        zr = sb("zr", [R, CH, HC])
        sd = sb("sd", [R, CH, HC, R])
        pr = sb("pr", [R, CH, HC, R])
        prt = sb("prt", [R, CH, HC, R + DH + 1])
        hall = sb("hall", [R, T, D])
        uall = sb("uall", [R, T, D])
        big = sb("big", [128, GROUPS * R])
        gall = big[0:R, :].rearrange("p (g n) -> p g n", n=R)
        avall = sb("avall", [R, GROUPS, DH + 2])
        comball = sb("comball", [R, T, E])
        red = sb("red", [R, 2])
        redall = sb("redall", [R, 2])
        cc = sb("cc", [R, 1])
        cinv = sb("cinv", [R, 1])
        X = [sb(f"x_{s}", [R, HC, R]) for s in range(CH)]
        P = [sb(f"p_{s}", [R, HC, R]) for s in range(CH)]
        Y = [sb(f"y_{s}", [R, HC, R]) for s in range(CH)]
        W = [sb(f"w_{s}", [R, HC, R]) for s in range(CH)]
        nos = sb("nos", [R, D])
        nrm2 = sb("nrm2", [R, D])
        stats2 = sb("stats2", [R, 6])
        mv2 = sb("mv2", [R, 2])
        veps2 = sb("veps2", [R, 1])
        rstd2 = sb("rstd2", [R, 1])
        aot = [sb(f"aot{k}", [128, R]) for k in range(2)]
        aos = sb("aos", [R, D])
        xps = sb("xps", [R, D])
        xmt = [sb(f"xmt{k}", [128, R]) for k in range(2)]
        xmall = [sb(f"xmall{k}", [128, T * R]) for k in range(2)]
        lg = sb("lg", [R, 2 * E])
        top8 = sb("top8", [R, 8])
        top2 = sb("top2", [R, 8])
        lrep = sb("lrep", [R, 2 * E])
        sel = sb("sel", [R, E])
        lsh = sb("lsh", [R, E])
        pe8 = sb("pe8", [R, E])
        psel = sb("psel", [R, E])
        psum1 = sb("psum1", [R, 1])
        pinv1 = sb("pinv1", [R, 1])
        cmb = sb("cmb", [R, E])
        cmbt = sb("cmbt", [E, R])
        w1t = [[sb(f"w1t{p}{k}", [128, DFF]) for k in range(2)] for p in range(2)]
        w2t = [sb(f"w2t{p}", [128, FC, D]) for p in range(2)]
        ht = [big[:, p * FC * NB * R:(p + 1) * FC * NB * R].rearrange("p (f n) -> p f n", f=FC) for p in range(2)]

        bank = [psum(f"bank{i}", [128, 512]) for i in range(8)]
        scp, btp, gp, avp, f0, f1 = bank[0:3], bank[3], bank[4], bank[5], bank[6], bank[7]
        inv_bank, f = bank[0:3], bank[3:8]
        h_bank, y_bank = [*bank[0:3], f1], [*bank[3:6], f0]

        consts_in = sem("consts_in")
        weights_in = sem("weights_in")
        patches_in = sem("patches_in")
        out_done = sem("out_done")
        fixed = sem("fixed")
        bias_ps = sem("bias_ps")
        post_done = sem("post_done")

        lin_ps, var_done, rstd_done, norm_done = sem("lin_ps"), sem("var_done"), sem("rstd_done"), sem("norm_done")
        xt_ps, xt_sb, q_ps, k_ps, v_ps = sem("xt_ps"), sem("xt_sb"), sem("q_ps"), sem("k_ps"), sem("v_ps")
        q_sb, k_sb, v_sb = sem("q_sb"), sem("k_sb"), sem("v_sb")
        prt_ps, prt_sb, av_sb = sem("prt_ps"), sem("prt_sb"), sem("av_sb")
        dve_step, pool_step = sem("dve_step"), sem("pool_step")
        sc_ps, g_ps = sems("sc_ps", CH), sems("g_ps", CH)
        sub_done, exp_done, pr_done = sems("sub_done", CH), sems("exp_done", CH), sems("pr_done", CH)
        red_done, redall_done, cinv_step = sem("red_done"), sem("redall_done"), sem("cinv_step")
        x_done, x74_done, y_done = sems("x_done", CH), sems("x74_done", CH), sems("y_done", CH)
        p_done, w_done, half_ps = sems("p_done", CH), sems("w_done", CH), sems("half_ps", CH)
        n_ps, nos_sb = sems("n_ps", CH), sems("nos_sb", CH)
        a_not_ps, a_not_sb, a_proj_ps = sem("a_not_ps"), sem("a_not_sb"), sem("a_proj_ps")
        a_var, a_rstd, a_pool, a_step = sem("a_var"), sem("a_rstd"), sem("a_pool"), sem("a_step")
        a_norm, a_xt_ps, a_xt_sb = sem("a_norm"), sem("a_xt_ps"), sem("a_xt_sb")
        a_q_ps, a_k_ps, a_v_ps = sem("a_q_ps"), sem("a_k_ps"), sem("a_v_ps")
        a_q_sb, a_k_sb, a_v_sb = sem("a_q_sb"), sem("a_k_sb"), sem("a_v_sb")
        a_sc_ps, a_sub, a_exp, a_prt_ps, a_prt_sb = sem("a_sc_ps"), sem("a_sub"), sem("a_exp"), sem("a_prt_ps"), sem("a_prt_sb")
        b_av_ps, b_ao, b_aot_ps, b_aot_sb, b_mix_ps = sem("b_av_ps"), sem("b_ao"), sem("b_aot_ps"), sem("b_aot_sb"), sem("b_mix_ps")
        b_xp, b_acc, b_var, b_rstd, b_pool, b_step = sem("b_xp"), sem("b_acc"), sem("b_var"), sem("b_rstd"), sem("b_pool"), sem("b_step")
        b_norm, b_xmt_ps, b_xmt_sb, b_xmall = sem("b_norm"), sem("b_xmt_ps"), sem("b_xmt_sb"), sem("b_xmall")
        b_router_ps, b_lg, b_lsh, b_pe8 = sem("b_router_ps"), sem("b_lg"), sem("b_lsh"), sem("b_pe8")
        c_step = sem("c_step")
        c_cmb, c_cmbt_ps, c_cmbt_sb, c_b2_ps, c_b2 = sem("c_cmb"), sem("c_cmbt_ps"), sem("c_cmbt_sb"), sem("c_b2_ps"), sem("c_b2")
        expert_in = sems("expert_in", 2)
        h_ps = sem("h_ps")
        gelu_done = sems("gelu_done", 4)
        y_ps = sems("y_ps", 2)
        y_used = sems("y_used", 4)

        BLOCKS = [(0, 3), (3, 3), (6, 3), (9, 2)]
        Y_USES = [len([j for j in range(T) if j % 4 == b]) for b in range(4)]
        Y_TILES = [[j for k in (b, b + 2) for j in range(BLOCKS[k][0], sum(BLOCKS[k]))] for b in range(2)]

        started = sem("started")

        primed = [prt_sb, av_sb, v_sb, k_sb, *sub_done, *exp_done, *g_ps, *n_ps, *nos_sb, *x_done, *half_ps,
                  *gelu_done, *y_ps, *y_used]

        def at(semaphore, count):
            count = count + 1 if any(semaphore is x for x in primed) else count
            return max(count, 0) if isinstance(count, int) else count

        def gate(eng):
            eng.nop(nofuse=True)

        block = ctx.enter_context(nc.Block())

        def heads(b, n, m=HC):
            return b[0:R, 0:m * n].rearrange("p (j n) -> p j n", n=n)

        def rounds(eng, one):
            for g in range(3):
                one(g, True, g >= 1, g >= 2, False)
            with eng.Fori(3, T) as g:
                one(g, True, True, True, True)
            for g in range(T, T + 3):
                one(g, False, g < T + 1, g < T + 2, True)

        class Chain:

            def __init__(self, eng, sem_):
                self.eng, self.sem, self.base, self.n = eng, sem_, 0, 0

            def done(self, ins):
                self.n += 1
                ins.then_inc(self.sem, 1)

            def wait(self):
                self.eng.wait_ge(self.sem, at(self.sem, self.base + self.n))

        @block.sync
        def _(sp):
            sp.dma_start(pt[:, :], patches[:, 0, :]).then_inc(patches_in, 16)
            sp.dma_start(wtok[:, :, :], w_tok).then_inc(consts_in, 16)
            sp.dma_start(cst[:, :], consts).then_inc(consts_in, 16)
            sp.dma_start(btok[:, :], b_tok).then_inc(consts_in, 16)
            sp.dma_start(rmask[:, :], row_mask).then_inc(consts_in, 16)
            sp.dma_start(post[:, :], pos).then_inc(consts_in, 16)
            sp.dma_start(xtb1[KB:AUG, :], aug1).then_inc(consts_in, 16)
            sp.dma_start(xtb2[KB:AUG, :], aug2).then_inc(consts_in, 16)
            for k, (lo, hi) in enumerate([(0, 128), (128, 128 + AUG)]):
                sp.dma_start(wqk[0][k][0:hi - lo, :, :], wqk1[lo:hi, :, :]).then_inc(consts_in, 16)
            for k, (lo, hi) in enumerate([(0, 128), (128, D)]):
                sp.dma_start(wv[0][k][0:hi - lo, :], wv1[lo:hi, :]).then_inc(consts_in, 16)
            with sp.Fori(1, T) as t:
                sp.wait_ge(lin_ps, at(lin_ps, t))
                sp.dma_start(pt[:, :], patches[:, t, :]).then_inc(patches_in, 16)
            for k, (lo, hi) in enumerate([(0, 128), (128, 128 + AUG)]):
                sp.dma_start(wqk[1][k][0:hi - lo, :, :], wqk2[lo:hi, :, :]).then_inc(weights_in, 16)
            for k, (lo, hi) in enumerate([(0, 128), (128, D + 1)]):
                for dst, src in ((wv[1], wv2), (wo[0], wproj1), (wo[1], wproj2), (wr, router)):
                    sp.dma_start(dst[k][0:hi - lo, :], src[lo:hi, :]).then_inc(weights_in, 16)
            sp.dma_start(b2t[:, :], b2).then_inc(weights_in, 16)
            sp.dma_start(aff[:, :], affine).then_inc(weights_in, 16)
            sp.dma_start(b1t[:, :, :], b1).then_inc(weights_in, 16)

            def load_expert(e, p):
                for k, (lo, hi) in enumerate([(0, 128), (128, D)]):
                    sp.dma_start(w1t[p][k][0:hi - lo, :], w1[e, lo:hi, :]).then_inc(expert_in[p], 16)
                sp.dma_start(w2t[p][:, :, :], w2[e, :, :].rearrange("p (c d) -> p c d", c=FC)).then_inc(expert_in[p], 16)

            for p in range(2):
                load_expert(p, p)
            with sp.Fori(1, E // 2) as i:
                for p in range(2):
                    for b in range(2):
                        sp.wait_ge(y_ps[b], at(y_ps[b], (2 * i + p - 1) * len(Y_TILES[b])))
                    load_expert(2 * i + p, p)
            for b in range(4):
                sp.wait_ge(y_used[b], at(y_used[b], E * Y_USES[b]))
            for b in range(NB):
                src = hall[b * S:b * S + TOK, 0:T - 1, :]
                dst = out[0:NB * (T - 1), :, :].rearrange("(t b) i d -> b i t d", b=NB)[b]
                sp.dma_start(dst, src).then_inc(out_done, 16)
            for b in range(NB * T - IMAGES, NB):
                sp.dma_start(out[FIRST_IMAGE[-1] + b, :, :], hall[b * S:b * S + TOK, T - 1, :]).then_inc(out_done, 16)
            sp.wait_ge(out_done, at(out_done, 16 * (NB + NB - (NB * T - IMAGES))))

        CONSTS_IN = 16 * 11
        WEIGHTS_IN = 16 * 13
        FIXED = 6

        @block.tensor
        def _(pe):
            mm = nc.tensor.matmul

            def tr(dst, src, n):
                return nc.tensor.transpose(dst, src, ident[0:n, 0:n])

            def to_features(src, b):
                tr(b[:, 0:R], src[:, 0:128], R)
                return tr(b[0:KB, R:2 * R], src[:, 128:D], R)

            def queries_or_keys(q, l, xb, dst):
                w = wqk[l]
                for c in range(CH):
                    mm(dst[:, c * R:(c + 1) * R], w[0][:, q, c * 128:(c + 1) * 128], xta[:, :], start=True, stop=False)
                    last = mm(dst[:, c * R:(c + 1) * R], w[1][0:AUG, q, c * 128:(c + 1) * 128], xb[0:AUG, :],
                              start=False, stop=True)
                return last

            def linear(src, w, k, dst, n=D):
                mm(dst[0:R, 0:n], src[0][:, :], w[0][:, :], start=True, stop=False)
                return mm(dst[0:R, 0:n], src[1][0:k, :], w[1][0:k, :], start=False, stop=True)

            def scores(c, dst):
                return mm(dst[0:R, 0:HC * R], qt[:, c * R:(c + 1) * R], ktm[:, c, :, :].rearrange("p j n -> p (j n)"),
                          start=True, stop=True)

            pe.wait_ge(consts_in, at(consts_in, CONSTS_IN))
            mm(f0[0:R, 0:D], rmask[0:1, :], btok[0:1, :], start=True, stop=True).then_inc(bias_ps, 1)

            def embed(t):
                pe.wait_ge(patches_in, at(patches_in, 16 * (t + 1)))
                pe.wait_ge(v_sb, at(v_sb, t))
                for k in range(PC):
                    last = mm(f0[0:R, 0:D], pt[:, k * R:(k + 1) * R], wtok[:, k, :], start=(k == 0), stop=(k == PC - 1))
                last.then_inc(lin_ps, 1)

            def hidden_to_features(t):
                pe.wait_ge(norm_done, at(norm_done, t + 1))
                pe.wait_ge(k_sb, at(k_sb, HC * t))
                to_features(nrm, f1).then_inc(xt_ps, 1)

            def qk1(t):
                pe.wait_ge(xt_sb, at(xt_sb, 2 * (t + 1)))
                queries_or_keys(0, 0, xtb1, f0).then_inc(q_ps, 1)
                queries_or_keys(1, 0, xtb1, f1).then_inc(k_ps, 1)

            def values1(t):
                pe.wait_ge(q_sb, at(q_sb, t + 1))
                linear([xta, xtb1], wv[0], KB, f0).then_inc(v_ps, 1)

            def scores1(t, c):
                if c == 0:
                    pe.wait_ge(q_sb, at(q_sb, t + 1))
                    pe.wait_ge(k_sb, at(k_sb, HC * (t + 1)))
                pe.wait_ge(sub_done[c], at(sub_done[c], t))
                scores(c, scp[c]).then_inc(sc_ps[c], 1)

            def transpose1(t, c):
                pe.wait_ge(pr_done[c], at(pr_done[c], t + 1))
                pe.wait_ge(prt_sb, at(prt_sb, CH * t + c))
                for j in range(HC):
                    last = mm(btp[0:R, j * (R + 1):(j + 1) * (R + 1)], pr[:, c, j, :], idw, start=True, stop=True)
                last.then_inc(prt_ps, 1)

            def gram(t, c):
                pe.wait_ge(prt_sb, at(prt_sb, CH * t + c + 1))
                pe.wait_ge(av_sb, at(av_sb, CH * t + c))
                if c == 0:
                    pe.wait_ge(v_sb, at(v_sb, t + 1))
                n = R + DH + 1
                for j in range(HC):
                    b = (gp, avp)[j // 2]
                    last = mm(b[0:R, j % 2 * n:(j % 2 + 1) * n], prt[:, c, j, 0:R], prt[:, c, j, :], start=True, stop=True)
                last.then_inc(g_ps[c], 1)

            def tile1(t, nxt):
                for c in range(CH):
                    scores1(t, c)
                if nxt is not None:
                    embed(nxt)
                transpose1(t, 0)
                gram(t, 0)
                if nxt is not None:
                    hidden_to_features(nxt)
                    qk1(nxt)
                transpose1(t, 1)
                gram(t, 1)
                transpose1(t, 2)
                gram(t, 2)
                if nxt is not None:
                    values1(nxt)

            pe.wait_ge(post_done, at(post_done, 1))
            embed(0)
            hidden_to_features(0)
            qk1(0)
            values1(0)
            with pe.Fori(0, T - 1) as t:
                tile1(t, t + 1)
            tile1(T - 1, None)

            pe.wait_ge(weights_in, at(weights_in, WEIGHTS_IN))

            def half_step(g, k):
                n = k // 2
                for s in range(CH):
                    if k % 2 == 0:
                        pe.wait_ge(x_done[s], at(x_done[s], 7 * g + n + 1))
                        if n == 0:
                            pe.wait_ge(nos_sb[s], at(nos_sb[s], g))
                        left, right = X[s], X[s]
                    else:
                        pe.wait_ge(p_done[s], at(p_done[s], ITERS * g + n + 1))
                        pe.wait_ge(w_done[s], at(w_done[s], ITERS * g + n + 1))
                        left, right = P[s], W[s]
                    for j in range(HC):
                        last = mm(inv_bank[s][0:R, j * R:(j + 1) * R], left[:, j, :], right[:, j, :], start=True, stop=True)
                    last.then_inc(half_ps[s], 1)

            def apply_inverse(g):
                for s in range(CH):
                    pe.wait_ge(x_done[s], at(x_done[s], 7 * g + 7))
                    for j in range(HC):
                        last = mm(inv_bank[s][0:R, j * DH:(j + 1) * DH], X[s][:, j, :],
                                  avall[:, g * H + (s * HC + j), 0:DH], start=True, stop=True)
                    last.then_inc(n_ps[s], 1)

            def transpose2(t, c):
                pe.wait_ge(a_exp, at(a_exp, CH * t + c + 1))
                for j in range(HC):
                    last = tr(f[2][0:R, j * R:(j + 1) * R], pr[:, c, j, :], R)
                last.then_inc(a_prt_ps, 1)

            def attend(t, c):
                pe.wait_ge(a_prt_sb, at(a_prt_sb, CH * t + c + 1))
                for j in range(HC):
                    last = mm(f[3][0:R, j * (DH + 1):(j + 1) * (DH + 1)], prt[:, c, j, 0:R], v1[:, c * HC + j, :],
                              start=True, stop=True)
                last.then_inc(b_av_ps, 1)

            def stage_a(t, k):
                if k == 0:
                    for s in range(CH):
                        pe.wait_ge(nos_sb[s], at(nos_sb[s], t + 1))
                    pe.wait_ge(b_lg, at(b_lg, t - 1))
                    to_features(nos, f[0]).then_inc(a_not_ps, 1)
                if k == 1:
                    pe.wait_ge(a_not_sb, at(a_not_sb, 2 * (t + 1)))
                    pe.wait_ge(b_xmt_sb, at(b_xmt_sb, 2 * (t - 1)))
                    linear(aot, wo[0], KB + 1, f[1]).then_inc(a_proj_ps, 1)
                if k == 5:
                    pe.wait_ge(a_norm, at(a_norm, t + 1))
                    to_features(nrm, f[0]).then_inc(a_xt_ps, 1)
                if k == 6:
                    pe.wait_ge(a_xt_sb, at(a_xt_sb, 2 * (t + 1)))
                    pe.wait_ge(a_prt_sb, at(a_prt_sb, CH * t))
                    queries_or_keys(0, 1, xtb2, f[2]).then_inc(a_q_ps, 1)
                    pe.wait_ge(b_ao, at(b_ao, CH * t))
                    queries_or_keys(1, 1, xtb2, f[3]).then_inc(a_k_ps, 1)
                if k == 7:
                    pe.wait_ge(a_q_sb, at(a_q_sb, t + 1))
                    linear([xta, xtb2], wv[1], KB + 1, f[2]).then_inc(a_v_ps, 1)
                if k == 8:
                    pe.wait_ge(a_k_sb, at(a_k_sb, HC * (t + 1)))
                    scores(0, f[3]).then_inc(a_sc_ps, 1)
                if k == 9:
                    pe.wait_ge(c_b2, at(c_b2, t - 1))
                    scores(1, f[4]).then_inc(a_sc_ps, 1)
                if k == 10:
                    pe.wait_ge(a_sub, at(a_sub, CH * t + 1))
                    scores(2, f[3]).then_inc(a_sc_ps, 1)
                if k == 11:
                    pe.wait_ge(a_v_sb, at(a_v_sb, t + 1))
                    transpose2(t, 0)

            def stage_b(t, k):
                if k < 2:
                    pe.wait_ge(a_prt_sb, at(a_prt_sb, CH * t + k + 1))
                    transpose2(t, k + 1)
                if k == 1:
                    pe.wait_ge(a_sub, at(a_sub, CH * t + CH))
                    attend(t, 0)
                if k in (2, 3):
                    pe.wait_ge(b_ao, at(b_ao, CH * t + k - 1))
                    attend(t, k - 1)
                if k == 5:
                    pe.wait_ge(b_ao, at(b_ao, CH * (t + 1)))
                    to_features(aos, f[1]).then_inc(b_aot_ps, 1)
                if k == 6:
                    pe.wait_ge(b_aot_sb, at(b_aot_sb, 2 * (t + 1)))
                    linear(aot, wo[1], KB + 1, f[0]).then_inc(b_mix_ps, 1)
                if k == 9:
                    pe.wait_ge(b_norm, at(b_norm, t + 1))
                    to_features(nrm2, f[1]).then_inc(b_xmt_ps, 1)
                if k == 10:
                    pe.wait_ge(b_xmt_sb, at(b_xmt_sb, 2 * (t + 1)))
                    linear(xmt, wr, KB + 1, f[0], E).then_inc(b_router_ps, 1)

            def stage_c(t, k):
                if k == 1:
                    pe.wait_ge(c_cmb, at(c_cmb, t + 1))
                    pe.wait_ge(a_sub, at(a_sub, min(CH * (t + 1) + 2, CH * T) if isinstance(t, int) else CH * (t + 1) + 2))
                    tr(f[4][0:E, 0:R], cmb[:, :], R).then_inc(c_cmbt_ps, 1)
                if k == 2:
                    pe.wait_ge(c_cmbt_sb, at(c_cmbt_sb, t + 1))
                    mm(f[4][0:R, 0:D], cmbt[:, :], b2t[:, :], start=True, stop=True).then_inc(c_b2_ps, 1)

            def one(g, inverse, a, b, c):
                for k in range(SLOTS):
                    if inverse:
                        half_step(g, k)
                    if a:
                        stage_a(g - 1, k)
                    if b:
                        stage_b(g - 2, k)
                    if c:
                        stage_c(g - 3, k)
                if inverse:
                    apply_inverse(g)

            rounds(pe, one)

            pe.wait_ge(b_xmall, at(b_xmall, 2 * T))
            pe.wait_ge(c_b2, at(c_b2, T))

            def hidden(e, p, blk):
                t0, nt = BLOCKS[blk]
                cols = slice(t0 * R, (t0 + nt) * R)
                for f in range(FC):
                    i = blk * FC + f
                    pe.wait_ge(gelu_done[i % 4], at(gelu_done[i % 4], e * FC + i // 4))
                    dst = h_bank[i % 4][:, 0:nt * R]
                    mm(dst, w1t[p][0][:, f * 128:(f + 1) * 128], xmall[0][:, cols], start=True, stop=False)
                    mm(dst, w1t[p][1][0:KB, f * 128:(f + 1) * 128], xmall[1][0:KB, cols],
                       start=False, stop=True).then_inc(h_ps, 1)

            def down(e, p, blk):
                t0, nt = BLOCKS[blk]
                for t in range(t0, t0 + nt):
                    pe.wait_ge(y_used[t % 4], at(y_used[t % 4], e * Y_USES[t % 4] + t // 4))
                    for f in range(FC):
                        if t == t0:
                            i = blk * FC + f
                            pe.wait_ge(gelu_done[i % 4], at(gelu_done[i % 4], e * FC + i // 4 + 1))
                        last = mm(y_bank[t % 4][0:R, 0:D], ht[blk % 2][:, f, (t - t0) * R:(t - t0 + 1) * R],
                                  w2t[p][:, f, :], start=(f == 0), stop=(f == FC - 1))
                    last.then_inc(y_ps[blk % 2], 1)

            with pe.Fori(0, E // 2) as i:
                for p in range(2):
                    e = 2 * i + p
                    pe.wait_ge(expert_in[p], at(expert_in[p], 48 * (i + 1)))
                    hidden(e, p, 0)
                    hidden(e, p, 1)
                    down(e, p, 0)
                    hidden(e, p, 2)
                    down(e, p, 1)
                    hidden(e, p, 3)
                    down(e, p, 2)
                    down(e, p, 3)

        @block.scalar
        def _(act):
            def copy(dst, src):
                return nc.scalar.activation(dst, src, ACT.Copy)

            def affine_out(dst, src, k, which):
                n = 128 if k == 0 else KB
                c = 4 * k + 2 * which
                return nc.scalar.activation(dst, src, ACT.Identity, bias=aff[0:n, c + 1:c + 2], scale=aff[0:n, c:c + 1])

            def keys_out(src, done):
                for j in range(0, 2):
                    q = slice(32 * j, 32 * j + 32)
                    copy(ktm[q, :, j, :], src[q, 0:CH * R].rearrange("p (c n) -> p c n", n=R)).then_inc(done, 1)

            def by_head(ap):
                return ap.rearrange("p (h d) -> p h d", d=DH)

            def xt_out(t):
                act.wait_ge(xt_ps, at(xt_ps, t + 1))
                copy(xta[:, :], f1[:, 0:R]).then_inc(xt_sb, 1)
                copy(xtb1[0:KB, :], f1[0:KB, R:2 * R]).then_inc(xt_sb, 1)

            def qk_out(t):
                act.wait_ge(q_ps, at(q_ps, t + 1))
                copy(qt[:, :], f0[:, 0:CH * R]).then_inc(q_sb, 1)
                act.wait_ge(k_ps, at(k_ps, t + 1))
                act.wait_ge(fixed, at(fixed, FIXED))
                keys_out(f1, k_sb)

            def v_out(t):
                act.wait_ge(v_ps, at(v_ps, t + 1))
                copy(prt[:, :, :, R:R + DH].rearrange("p c j d -> p (c j) d"), by_head(f0[0:R, 0:D])).then_inc(v_sb, 1)

            def exp1(t, c):
                act.wait_ge(sub_done[c], at(sub_done[c], t + 1))
                act.wait_ge(g_ps[c], at(g_ps[c], t))
                nc.scalar.activation(pr[:, c], sd[:, c], ACT.Exp, scale=DH ** -0.5).then_inc(exp_done[c], 1)

            def prt_out(t, c):
                act.wait_ge(prt_ps, at(prt_ps, CH * t + c + 1))
                gate(act)
                src = heads(btp, R + 1)
                copy(avall[:, bass.ds(t * H + c * HC, HC), DH + 1:DH + 2], src[:, :, R:R + 1])
                copy(prt[:, c, :, 0:R], src[:, :, 0:R]).then_inc(prt_sb, 1)

            def gram_out(t, c):
                act.wait_ge(g_ps[c], at(g_ps[c], t + 1))
                gate(act)
                for i, b in enumerate((gp, avp)):
                    src = heads(b, R + DH + 1, 2)
                    copy(gall[:, bass.ds(t * H + (c * HC + 2 * i), 2), :], src[:, :, 0:R])
                    last = copy(avall[:, bass.ds(t * H + (c * HC + 2 * i), 2), 0:DH + 1], src[:, :, R:R + DH + 1])
                last.then_inc(av_sb, 1)

            def tile1(t, nxt):
                for c in range(CH):
                    exp1(t, c)
                prt_out(t, 0)
                gram_out(t, 0)
                if nxt is not None:
                    xt_out(nxt)
                    qk_out(nxt)
                prt_out(t, 1)
                gram_out(t, 1)
                prt_out(t, 2)
                gram_out(t, 2)
                if nxt is not None:
                    v_out(nxt)

            xt_out(0)
            qk_out(0)
            v_out(0)
            with act.Fori(0, T - 1) as t:
                tile1(t, t + 1)
            tile1(T - 1, None)

            act.wait_ge(weights_in, at(weights_in, WEIGHTS_IN))

            def x74(s, count):
                act.wait_ge(x_done[s], at(x_done[s], count))
                nc.scalar.activation(Y[s][:, :, :], X[s][:, :, :], ACT.Copy, scale=1.75).then_inc(x74_done[s], 1)

            def half_step(g, k):
                n = k // 2
                for s in range(CH):
                    if k % 2 == 0:
                        act.wait_ge(half_ps[s], at(half_ps[s], SLOTS * g + k + 1))
                        copy(P[s][:, :, :], heads(inv_bank[s], R)).then_inc(p_done[s], 1)
                    elif n < ITERS - 1:
                        x74(s, 7 * g + n + 2)

            def features_out(dst, src, done):
                copy(dst[0][:, :], src[:, 0:R]).then_inc(done, 1)
                copy(dst[1][0:KB, :], src[0:KB, R:2 * R]).then_inc(done, 1)

            def affine_out2(dst, src, done, which):
                affine_out(dst[0][:, :], src[:, 0:R], 0, which).then_inc(done, 1)
                affine_out(dst[1][0:KB, :], src[0:KB, R:2 * R], 1, which).then_inc(done, 1)

            def transpose_out(t, c):
                act.wait_ge(a_prt_ps, at(a_prt_ps, CH * t + c + 1))
                copy(prt[:, c, :, 0:R], heads(f[2], R)).then_inc(a_prt_sb, 1)

            def stage_a(t, k):
                if k == 0:
                    act.wait_ge(a_not_ps, at(a_not_ps, t + 1))
                    features_out(aot, f[0], a_not_sb)
                if k == 5:
                    act.wait_ge(a_xt_ps, at(a_xt_ps, t + 1))
                    affine_out2([xta, xtb2], f[0], a_xt_sb, 0)
                if k == 6:
                    act.wait_ge(a_q_ps, at(a_q_ps, t + 1))
                    copy(qt[:, :], f[2][:, 0:CH * R]).then_inc(a_q_sb, 1)
                    act.wait_ge(a_k_ps, at(a_k_ps, t + 1))
                    keys_out(f[3], a_k_sb)
                if k == 7:
                    act.wait_ge(a_v_ps, at(a_v_ps, t + 1))
                    copy(v1[:, :, 0:DH], by_head(f[2][0:R, 0:D])).then_inc(a_v_sb, 1)
                if 9 <= k:
                    c = k - 9
                    act.wait_ge(a_sub, at(a_sub, CH * t + c + 1))
                    nc.scalar.activation(pr[:, c], sd[:, c], ACT.Exp, scale=DH ** -0.5).then_inc(a_exp, 1)
                if k == 11:
                    transpose_out(t, 0)

            def stage_b(t, k):
                if k < 2:
                    transpose_out(t, k + 1)
                if k == 5:
                    act.wait_ge(b_aot_ps, at(b_aot_ps, t + 1))
                    features_out(aot, f[1], b_aot_sb)
                if k == 9:
                    act.wait_ge(b_xmt_ps, at(b_xmt_ps, t + 1))
                    act.wait_ge(b_xmall, at(b_xmall, 2 * t))
                    affine_out2(xmt, f[1], b_xmt_sb, 1)
                if k == 11:
                    act.wait_ge(b_lsh, at(b_lsh, t + 1))
                    nc.scalar.activation(pe8[:, :], lsh[:, :], ACT.Exp).then_inc(b_pe8, 1)

            def stage_c(t, k):
                if k == 1:
                    act.wait_ge(c_cmbt_ps, at(c_cmbt_ps, t + 1))
                    copy(cmbt[:, :], f[4][0:E, 0:R]).then_inc(c_cmbt_sb, 1)

            def one(g, inverse, a, b, c):
                if inverse:
                    for s in range(CH):
                        x74(s, 7 * g + 1)
                for k in range(SLOTS):
                    if inverse:
                        half_step(g, k)
                    if a:
                        stage_a(g - 1, k)
                    if b:
                        stage_b(g - 2, k)
                    if c:
                        stage_c(g - 3, k)
                if inverse:
                    for s in range(CH):
                        act.wait_ge(n_ps[s], at(n_ps[s], g + 1))
                        copy(nos[:, s * HC * DH:(s + 1) * HC * DH], inv_bank[s][0:R, 0:HC * DH]).then_inc(nos_sb[s], 1)

            rounds(act, one)

            def gelus(e, blk):
                nt = BLOCKS[blk][1]
                for f in range(FC):
                    i = blk * FC + f
                    act.wait_ge(h_ps, at(h_ps, e * FC * 4 + i + 1))
                    if f == 0:
                        act.wait_ge(y_ps[blk % 2], at(y_ps[blk % 2], e * len(Y_TILES[blk % 2]) + (3 if blk > 1 else 0)))
                    gate(act)
                    nc.scalar.activation(ht[blk % 2][:, f, 0:nt * R], h_bank[i % 4][:, 0:nt * R], ACT.Gelu,
                                         bias=b1t[:, e, f:f + 1]).then_inc(gelu_done[i % 4], 1)

            with act.Fori(0, E // 2) as i:
                for p in range(2):
                    for blk in range(4):
                        gelus(2 * i + p, blk)

        @block.vector
        def _(dve):
            V = nc.vector

            def norm_stats(ch, st, m, src, var_sem):
                ch.wait()
                gate(dve)
                ch.done(V.bn_stats(st[:, :], src))
                ch.wait()
                gate(dve)
                V.bn_aggr(m[:, :], st[:, :]).then_inc(var_sem, 1)

            def wide(ap):
                return ap.unsqueeze(2).to_broadcast([R, HC, R])

            def shift(ch, c, src, done):
                ch.done(V.tensor_reduce(mx[:, c, :], heads(src, R), axis=AX.X, op=ALU.max))
                ch.wait()
                V.tensor_tensor(sd[:, c], heads(src, R), wide(mx[:, c, :]), ALU.subtract).then_inc(done, 1)

            def keys_out(src, done):
                for j in range(2, HC):
                    q = slice(32 * j, 32 * j + 32)
                    V.tensor_copy(ktm[q, :, j, :], src[q, 0:CH * R].rearrange("p (c n) -> p c n", n=R)).then_inc(done, 1)

            dve.wait_ge(consts_in, at(consts_in, CONSTS_IN))
            V.memset(ktm[:, :, :, :], 0.0).then_inc(fixed, 1)
            V.tensor_copy(prt[:, :, :, R + DH].rearrange("p c j -> p (c j)"), wcol.to_broadcast([R, H])).then_inc(fixed, 1)
            V.memset(v1[:, :, DH:DH + 1], 1.0).then_inc(fixed, 1)
            V.memset(aot[1][KB:KB + 1, :], 1.0).then_inc(fixed, 1)
            V.memset(xmt[1][KB:KB + 1, :], 1.0).then_inc(fixed, 1)
            V.memset(lg[:, E:2 * E], -3.0e38).then_inc(fixed, 1)
            dve.wait_ge(fixed, at(fixed, FIXED))
            dve.wait_ge(bias_ps, at(bias_ps, 1))
            V.tensor_tensor(post[:, :], post[:, :], f0[0:R, 0:D], ALU.add).then_inc(post_done, 1)
            dve.wait_ge(post_done, at(post_done, 1))

            c1 = Chain(dve, dve_step)

            def front1_a(t):
                dve.wait_ge(lin_ps, at(lin_ps, t + 1))
                c1.done(V.tensor_tensor(hall[:, t, :], f0[0:R, 0:D], post[:, :], ALU.add))
                norm_stats(c1, stats, mv, hall[:, t, :], var_done)

            def front1_b(t):
                dve.wait_ge(rstd_done, at(rstd_done, t + 1))
                V.tensor_scalar(nrm[:, :], hall[:, t, :], mv[:, 0:1], rstd[:, :], ALU.subtract, ALU.mult).then_inc(norm_done, 1)

            def k_out(t):
                dve.wait_ge(k_ps, at(k_ps, t + 1))
                keys_out(f1, k_sb)

            def shift1(t, c):
                dve.wait_ge(sc_ps[c], at(sc_ps[c], t + 1))
                dve.wait_ge(exp_done[c], at(exp_done[c], t))
                shift(c1, c, scp[c], sub_done[c])

            def softmax_norm(t, c):
                dve.wait_ge(exp_done[c], at(exp_done[c], t + 1))
                pads = pr[:, c].rearrange("p j (b n) -> p j b n", n=S)[:, :, :, S - 1]
                c1.done(V.tensor_reduce(zs[:, c, :], pr[:, c], axis=AX.X, op=ALU.add))
                c1.done(V.tensor_reduce(zp[:, c, :], pads, axis=AX.X, op=ALU.add))
                c1.wait()
                c1.done(V.scalar_tensor_tensor(zr[:, c, :], zp[:, c, :], float(PADS - 1), zs[:, c, :], ALU.mult, ALU.add))
                c1.wait()
                c1.done(V.reciprocal(zs[:, c, :], zr[:, c, :]))
                c1.wait()
                c1.done(V.tensor_scalar(zr[:, c, :], zs[:, c, :], wcol, None, ALU.mult))
                c1.wait()
                c1.done(V.tensor_tensor(pr[:, c], pr[:, c], wide(zr[:, c, :]), ALU.mult))
                c1.wait()
                V.tensor_scalar(pads, pads, ROOT, None, ALU.mult).then_inc(pr_done[c], 1)

            front1_a(0)
            front1_b(0)
            k_out(0)
            BEFORE = c1.n
            PER_TILE = BEFORE + CH * (1 + 6)

            def tile1(t, nxt):
                c1.base, c1.n = t * PER_TILE + BEFORE, 0
                for c in range(CH):
                    shift1(t, c)
                softmax_norm(t, 0)
                if nxt is not None:
                    front1_a(nxt)
                softmax_norm(t, 1)
                if nxt is not None:
                    front1_b(nxt)
                softmax_norm(t, 2)
                if nxt is not None:
                    k_out(nxt)
                    assert c1.n == PER_TILE

            with dve.Fori(0, T - 1) as t:
                tile1(t, t + 1)
            tile1(T - 1, None)

            dve.wait_ge(av_sb, at(av_sb, CH * T))
            c2 = Chain(dve, cinv_step)
            c2.done(V.tensor_reduce(red[:, :], avall[:, :, DH:DH + 2].rearrange("p g n -> p n g"), axis=AX.X, op=ALU.max))
            c2.wait()
            V.tensor_scalar(red[:, :], red[:, :], winv, None, ALU.mult).then_inc(red_done, 1)
            dve.wait_ge(redall_done, at(redall_done, 1))
            c2.done(V.tensor_tensor(cc[:, :], redall[:, 0:1], redall[:, 1:2], ALU.mult))
            c2.wait()
            c2.done(V.reciprocal(cinv[:, :], cc[:, :]))
            c2.wait()

            ca, cb = Chain(dve, a_step), Chain(dve, b_step)

            def half_step(g, k):
                n = k // 2
                for s in range(CH):
                    if k % 2 == 0:
                        dve.wait_ge(p_done[s], at(p_done[s], ITERS * g + n + 1))
                        dve.wait_ge(y_done[s], at(y_done[s], ITERS * g + n + 1))
                        V.scalar_tensor_tensor(W[s][:, :, :], P[s][:, :, :], -0.25, Y[s][:, :, :], ALU.mult, ALU.add)\
                            .then_inc(w_done[s], 1)
                    else:
                        dve.wait_ge(half_ps[s], at(half_ps[s], SLOTS * g + k + 1))
                        V.scalar_tensor_tensor(X[s][:, :, :], X[s][:, :, :], 3.25, heads(inv_bank[s], R), ALU.mult, ALU.add)\
                            .then_inc(x_done[s], 1)

            def shift2(t, c, src):
                dve.wait_ge(a_sc_ps, at(a_sc_ps, CH * t + c + 1))
                shift(ca, c, src, a_sub)

            def attention_out(t, c):
                dve.wait_ge(b_av_ps, at(b_av_ps, CH * t + c + 1))
                av = heads(f[3], DH + 1)
                cb.done(V.reciprocal(zs[:, c, :].unsqueeze(2), av[:, :, DH:DH + 1]))
                cb.wait()
                V.tensor_tensor(aos[:, c * HC * DH:(c + 1) * HC * DH].rearrange("p (j d) -> p j d", d=DH),
                                av[:, :, 0:DH], zs[:, c, :].unsqueeze(2).to_broadcast([R, HC, DH]), ALU.mult).then_inc(b_ao, 1)

            def stage_a(t, k):
                if k == 1:
                    dve.wait_ge(a_proj_ps, at(a_proj_ps, t + 1))
                    ca.done(V.tensor_tensor(hall[:, t, :], hall[:, t, :], f[1][0:R, 0:D], ALU.add))
                    norm_stats(ca, stats, mv, hall[:, t, :], a_var)
                if k == 2:
                    dve.wait_ge(a_rstd, at(a_rstd, 2 * t + 1))
                    ca.done(V.tensor_scalar(uall[:, t, :], hall[:, t, :], mv[:, 0:1], rstd[:, :], ALU.subtract, ALU.mult))
                    norm_stats(ca, stats, mv, uall[:, t, :], a_var)
                if k == 4:
                    dve.wait_ge(a_rstd, at(a_rstd, 2 * t + 2))
                    V.tensor_scalar(nrm[:, :], uall[:, t, :], mv[:, 0:1], rstd[:, :], ALU.subtract, ALU.mult).then_inc(a_norm, 1)
                if k == 6:
                    dve.wait_ge(a_k_ps, at(a_k_ps, t + 1))
                    keys_out(f[3], a_k_sb)
                if k == 8:
                    shift2(t, 0, f[3])
                if k == 9:
                    shift2(t, 1, f[4])
                if k == 10:
                    shift2(t, 2, f[3])

            def stage_b(t, k):
                if k in (1, 2, 3):
                    attention_out(t, k - 1)
                if k == 6:
                    dve.wait_ge(b_mix_ps, at(b_mix_ps, t + 1))
                    V.tensor_tensor(xps[:, :], uall[:, t, :], f[0][0:R, 0:D], ALU.add).then_inc(b_xp, 1)
                    dve.wait_ge(b_xp, at(b_xp, t + 1))
                    norm_stats(cb, stats2, mv2, xps[:, :], b_var)
                if k == 8:
                    dve.wait_ge(b_rstd, at(b_rstd, t + 1))
                    V.tensor_scalar(nrm2[:, :], xps[:, :], mv2[:, 0:1], rstd2[:, :], ALU.subtract, ALU.mult).then_inc(b_norm, 1)
                if k == 11:
                    dve.wait_ge(b_router_ps, at(b_router_ps, t + 1))
                    V.tensor_copy(lg[:, 0:E], f[0][0:R, 0:E]).then_inc(b_lg, 1)
                    dve.wait_ge(b_lg, at(b_lg, t + 1))
                    gate(dve)
                    cb.done(V.max(top8[:, :], lg[:, 0:E]))
                    cb.wait()
                    V.tensor_scalar(lsh[:, :], lg[:, 0:E], top8[:, 0:1], None, ALU.subtract).then_inc(b_lsh, 1)
                    cb.done(V.tensor_copy(top2[:, 0:2], top8[:, 0:2]))
                    cb.done(V.tensor_copy(top2[:, 2:8], lg[:, E:E + 6]))
                    cb.wait()
                    gate(dve)
                    cb.done(V.match_replace(lrep[:, :], top2[:, :], lg[:, :], 3.0e38))
                    cb.wait()
                    cb.done(V.tensor_tensor(sel[:, :], lrep[:, 0:E], lg[:, 0:E], ALU.not_equal))

            def stage_c(t, k):
                if k == 0:
                    cc3 = Chain(dve, c_step)
                    cc3.base = t * 3
                    dve.wait_ge(b_step, at(b_step, (t + 1) * B_STEPS))
                    dve.wait_ge(b_pe8, at(b_pe8, t + 1))
                    cc3.done(V.tensor_tensor(psel[:, :], pe8[:, :], sel[:, :], ALU.mult))
                    cc3.wait()
                    cc3.done(V.tensor_reduce(psum1[:, :], psel[:, :], axis=AX.X, op=ALU.add))
                    cc3.wait()
                    cc3.done(V.reciprocal(pinv1[:, :], psum1[:, :]))
                    cc3.wait()
                    V.tensor_scalar(cmb[:, :], psel[:, :], pinv1[:, :], None, ALU.mult).then_inc(c_cmb, 1)
                    dve.wait_ge(c_cmb, at(c_cmb, t + 1))
                    V.tensor_copy(comball[:, t, :], cmb[:, :])
                if k == 2:
                    dve.wait_ge(c_b2_ps, at(c_b2_ps, t + 1))
                    dve.wait_ge(b_acc, at(b_acc, t + 1))
                    V.tensor_tensor(hall[:, t, :], hall[:, t, :], f[4][0:R, 0:D], ALU.add).then_inc(c_b2, 1)

            A_STEPS, B_STEPS = 1 + 1 + 1 + 1 + CH, CH + 1 + 5

            def one(g, inverse, a, b, c):
                ca.base, ca.n, cb.base, cb.n = (g - 1) * A_STEPS, 0, (g - 2) * B_STEPS, 0
                if inverse:
                    for s in range(CH):
                        dve.wait_ge(n_ps[s], at(n_ps[s], g))
                        V.tensor_scalar(X[s][:, :, :], gall[:, bass.ds(g * H + s * HC, HC), :], cinv[:, :], None, ALU.mult)\
                            .then_inc(x_done[s], 1)
                for k in range(SLOTS):
                    if inverse:
                        half_step(g, k)
                    if a:
                        stage_a(g - 1, k)
                    if b:
                        stage_b(g - 2, k)
                    if c:
                        stage_c(g - 3, k)
                assert not a or ca.n == A_STEPS
                assert not b or cb.n == B_STEPS

            rounds(dve, one)

            dve.wait_ge(c_b2, at(c_b2, T))
            with dve.Fori(0, E // 2) as i:
                for p in range(2):
                    e = 2 * i + p
                    for b in range(4):
                        dve.wait_ge(y_used[b], at(y_used[b], e * Y_USES[b]))
                    for j in range(T):
                        b = 0 if j in Y_TILES[0] else 1
                        dve.wait_ge(y_ps[b], at(y_ps[b], e * len(Y_TILES[b]) + Y_TILES[b].index(j) + 1))
                        V.scalar_tensor_tensor(hall[:, j, :], y_bank[j % 4][0:R, 0:D], comball[:, j, bass.ds(e, 1)], hall[:, j, :],
                                               ALU.mult, ALU.add).then_inc(y_used[j % 4], 1)

        @block.gpsimd
        def _(pool):
            G = nc.gpsimd
            for x in primed:
                pool.sem_inc(x, 1)
            pool.sem_inc(started, 1)
            pool.wait_ge(consts_in, at(consts_in, CONSTS_IN))

            def inv_sqrt(var_sem, m, ve, rs, count, step, done):
                pool.wait_ge(var_sem, at(var_sem, count))
                gate(pool)
                G.tensor_scalar(ve[:, :], m[:, 1:2], EPS, None, ALU.add).then_inc(step, 1)
                pool.wait_ge(step, at(step, count))
                G.tensor_tensor(rs[:, :], ve[:, :], half, ALU.pow).then_inc(done, 1)

            with pool.Fori(0, T) as t:
                inv_sqrt(var_done, mv, veps, rstd, t + 1, pool_step, rstd_done)

            pool.wait_ge(red_done, at(red_done, 1))
            G.partition_all_reduce(redall[:, :], red[:, :], R, bass.bass_isa.ReduceOp.max).then_inc(redall_done, 1)

            eye = neg_eye.unsqueeze(1).to_broadcast([R, HC, R])

            def finish_y(g, n):
                for s in range(CH):
                    pool.wait_ge(x74_done[s], at(x74_done[s], ITERS * g + n + 1))
                    G.tensor_tensor(Y[s][:, :, :], Y[s][:, :, :], eye, ALU.add).then_inc(y_done[s], 1)

            def stage_a(t, k):
                if k == 2:
                    for n in range(2):
                        inv_sqrt(a_var, mv, veps, rstd, 2 * t + n + 1, a_pool, a_rstd)

            def stage_b(t, k):
                if k == 6:
                    inv_sqrt(b_var, mv2, veps2, rstd2, t + 1, b_pool, b_rstd)
                    pool.wait_ge(b_xp, at(b_xp, t + 1))
                    G.tensor_tensor(hall[:, t, :], hall[:, t, :], xps[:, :], ALU.add).then_inc(b_acc, 1)
                if k == 10:
                    pool.wait_ge(b_xmt_sb, at(b_xmt_sb, 2 * (t + 1)))
                    for i in range(2):
                        n = (128, KB)[i]
                        G.tensor_copy(xmall[i][0:n, bass.ds(t * R, R)], xmt[i][0:n, :]).then_inc(b_xmall, 1)

            def one(g, inverse, a, b, c):
                if inverse:
                    finish_y(g, 0)
                for k in range(SLOTS):
                    if inverse and k % 2 == 1 and k < SLOTS - 1:
                        finish_y(g, k // 2 + 1)
                    if a:
                        stage_a(g - 1, k)
                    if b:
                        stage_b(g - 2, k)

            rounds(pool, one)


def kernel(**inputs):
    import concourse.bacc as bacc
    from concourse.bass_utils import run_bass_kernel_spmd

    a = {k: np.asarray(v) for k, v in inputs.items()}
    f = np.float32

    x = a["x"].reshape(IMAGES, GRID, PATCH, GRID, PATCH, 3).transpose(0, 1, 3, 2, 4, 5).reshape(IMAGES, GRID * GRID, PD)
    rows = np.zeros((T, NB, S, PD), f)
    for t in range(T):
        rows[t, :, 1:TOK] = x[FIRST_IMAGE[t]:FIRST_IMAGE[t] + NB]
    patches = rows.reshape(T, R, PC, 128).transpose(3, 0, 2, 1).reshape(128, T, PC * R)
    pos = np.zeros((NB, S, D), f)
    pos[:, 0:TOK] = a["L0_tok_emb_table"][0:TOK]
    w_tok = a["L0_tok_W"].reshape(PC, 128, D).transpose(1, 0, 2)

    consts = np.zeros((128, C_COLS), f)
    consts[:, C_ID:C_ID + 128] = np.eye(128, dtype=f)
    row_mask = np.zeros((1, NB, S), f)
    row_mask[:, :, 1:TOK] = 1
    aug = np.zeros((2, 7, NB, S), f)
    aug[:, 0] = 1
    consts[0:R, C_IDW:C_IDW + R] = np.eye(R, dtype=f)
    consts[0:R, C_NEG:C_NEG + R] = -3.75 * np.eye(R, dtype=f)
    for b in range(NB):
        aug[:, 1 + b, b] = 1
        aug[:, 4 + b] = MASK
        aug[:, 4 + b, b] = 0
    aug[1, 4:7, :, S - 1] = MASK
    consts[:, C_W] = consts[:, C_WINV] = 1
    consts[S - 1:R:S, C_W] = ROOT
    consts[:, C_IDW + R] = consts[:, C_W]
    consts[S - 1:R:S, C_WINV] = 1 / ROOT
    consts[:, C_HALF] = -0.5

    def qk_layout(w, bias):
        o = np.zeros((128 + AUG, 2, H, 32), f)
        for q in range(2):
            o[0:D, q, :, 0:DH] = w[q * D:(q + 1) * D].T.reshape(D, H, DH)
            if bias is not None:
                o[D, q, :, 0:DH] = bias[q * D:(q + 1) * D].reshape(H, DH)
            for b in range(NB):
                o[D + 1 + NB * q + b, q, :, DH + b] = 1
        return o.reshape(128 + AUG, 2, H * 32)

    def with_bias(w, bias):
        o = np.zeros((w.shape[1] + 1, w.shape[0]), f)
        o[:-1] = w.T
        o[-1] = bias
        return o

    wq, wi = a["L0_attn_w_qkv"], a["L0_ffn_in_proj_w"]
    bi = a["L0_ffn_in_proj_b"]
    affine = np.zeros((128, 8), f)
    for n, name in enumerate(("ln1_g", "ln1_b", "ln2_g", "ln2_b")):
        v = a["L0_ffn_" + name]
        affine[:, n] = v[0:128]
        affine[0:KB, 4 + n] = v[128:D]
    arrays = {
        "patches": patches, "pos": pos.reshape(R, D), "consts": consts,
        "aug1": aug[0].reshape(7, R), "aug2": aug[1].reshape(7, R),
        "w_tok": w_tok, "b_tok": a["L0_tok_b"].reshape(1, D), "row_mask": row_mask.reshape(1, R),
        "wqk1": qk_layout(wq, None), "wv1": wq[2 * D:].T, "wproj1": with_bias(a["L0_attn_w_proj"], a["L0_attn_b_proj"]),
        "wqk2": qk_layout(wi, bi), "wv2": with_bias(wi[2 * D:], bi[2 * D:]),
        "wproj2": with_bias(a["L0_ffn_out_proj_w"], a["L0_ffn_out_proj_b"]),
        "router": with_bias(a["L0_ffn_router_w"], a["L0_ffn_router_b"]),
        "w1": a["L0_ffn_w1"], "b1": a["L0_ffn_b1"].reshape(E, FC, 128).transpose(2, 0, 1),
        "w2": a["L0_ffn_w2"].reshape(E, FC, 128, D).transpose(0, 2, 1, 3).reshape(E, 128, FC * D),
        "b2": a["L0_ffn_b2"], "affine": affine,
    }
    arrays = {k: np.ascontiguousarray(v) for k, v in arrays.items()}
    nc = bacc.Bacc("TRN2", target_bir_lowering=False, num_devices=1)
    aps = {k: nc.dram_tensor(k, v.shape, F32, kind="ExternalInput").ap() for k, v in arrays.items()}
    out = nc.dram_tensor("out", (IMAGES, TOK, D), F32, kind="ExternalOutput").ap()
    build(nc, out=out, **aps)
    r = run_bass_kernel_spmd(nc, [arrays], core_ids=[0])
    return r.results[0]["out"]
```

```python
from contextlib import ExitStack

import numpy as np
import concourse.bass as bass
from concourse import mybir

F32 = mybir.dt.float32
F32R = mybir.dt.float32r
ALU = mybir.AluOpType
ACT = mybir.ActivationFunctionType
AX = mybir.AxisListType

IMAGES, GRID, PATCH, D = 32, 6, 16, 192
TOK = GRID * GRID + 1
PADS = 64 - TOK
S = TOK + 1
NB = 3
R = NB * S
T = -(-IMAGES // NB)
LEFT = IMAGES - NB * (T - 1)
TILE_IMAGES = [[NB * t + b if NB * t + b < IMAGES else IMAGES - 1 - b for b in range(NB)] for t in range(T)]
ROWS = [R] * (T - 1) + [LEFT * S]
PD = PATCH * PATCH * 3
PC = PD // 128
H, DH = 12, 16
HC, CH = 4, 3
KB = D - 128
AUG = KB + 7
GROUPS = T * H
ITERS = 6
SLOTS = 2 * ITERS
E, DFF = 8, 768
FC = DFF // 128
EPS = 1e-5
MASK = -(2.0 ** 40)
ROOT = float(np.float32(np.sqrt(PADS)))

C_ID, C_NEG, C_W, C_WINV, C_HALF = 0, 128, 242, 243, 244
C_COLS = 245


def build(nc, patches, pos, consts, aug1, aug2, w_tok, b_tok, row_mask, wqk1, wv1, wproj1, wqk2, wv2,
          wproj2, router, w1, b1, w2, b2, affine, out):
    with ExitStack() as ctx:
        early = ExitStack()
        first = ExitStack()

        def sb(name, shape, dtype=F32, stack=ctx):
            return stack.enter_context(nc.sbuf_tensor(name, shape, dtype))

        def psum(name, shape):
            return ctx.enter_context(nc.psum_tensor(name, shape, F32))

        def sem(name):
            return ctx.enter_context(nc.semaphore(name))

        def sems(name, n):
            return [sem(f"{name}{i}") for i in range(n)]

        cst = sb("cst", [128, C_COLS])
        ident = cst[:, C_ID:C_ID + 128]
        neg_eye = cst[0:R, C_NEG:C_NEG + R]
        wcol = cst[0:R, C_W:C_W + 1]
        winv = cst[0:R, C_WINV:C_WINV + 1]
        half = cst[0:R, C_HALF:C_HALF + 1]
        wqk_2 = [sb(f"wqk1{k}", [128, 2, CH * 128]) for k in range(2)]
        wv_2 = [sb(f"wv1{k}", [128, D]) for k in range(2)]
        wtok = sb("wtok", [128, PC, D], stack=first)
        btok = sb("btok", [1, D], stack=first)
        rmask = sb("rmask", [1, R], stack=first)
        post = sb("post", [R, D], stack=first)
        pt = sb("pt", [128, PC * R], stack=first)
        wqk = [[sb(f"wqk0{k}", [128, 2, CH * 128], stack=first) for k in range(2)], wqk_2]
        wv = [[sb(f"wv0{k}", [128, D], stack=first) for k in range(2)], wv_2]
        first.close()
        XF = [sb(f"xf_{s}", [R, HC, R]) for s in range(CH)]
        xm_hi = sb("xm_hi", [128, T * R], F32R)
        xm_lo = sb("xm_lo", [128, T * R], F32R)
        nos = sb("nos", [R, D])
        nrm2 = sb("nrm2", [R, D])
        aos = sb("aos", [R, D])
        wo = [[sb(f"wo{l}{k}", [128, D]) for k in range(2)] for l in range(2)]
        wr = [sb(f"wr{k}", [128, E]) for k in range(2)]
        b2t = sb("b2t", [E, D])
        aff = sb("aff", [128, 8])
        b1t = sb("b1t", [128, E, FC])

        nrm = sb("nrm", [R, D])
        stats = sb("stats", [R, 6])
        mv = sb("mv", [R, 2])
        veps = sb("veps", [R, 1])
        rstd = sb("rstd", [R, 1])
        xta = sb("xta", [128, R])
        xtb1 = sb("xtb1", [128, R])
        xtb2 = sb("xtb2", [128, R])
        qt = sb("qt", [128, CH * R])
        ktm = sb("ktm", [128, CH, HC, R])
        v1 = sb("v1", [R, H, DH + 1])
        mx = sb("mx", [R, CH, HC])
        zs = sb("zs", [R, CH, HC])
        zp = sb("zp", [R, CH, HC])
        zr = sb("zr", [R, CH, HC])
        sd = sb("sd", [R, CH, HC, R])
        pr = sb("pr", [R, CH, HC, R])
        prt = sb("prt", [R, CH, HC, R + DH + 1])
        hall = sb("hall", [R, T, D])
        uall = sb("uall", [R, T, D])
        avall = sb("avall", [R, GROUPS, DH + 1])
        csb = sb("csb", [R, H, S])
        cs = sb("cs", [R, H])
        csmax = sb("csmax", [R, H])
        comball = sb("comball", [R, T, E])
        red = sb("red", [R, 2])
        redall = sb("redall", [R, 2])
        cc = sb("cc", [R, 1])
        cinv = sb("cinv", [R, 1])
        stats2 = sb("stats2", [R, 6])
        mv2 = sb("mv2", [R, 2])
        veps2 = sb("veps2", [R, 1])
        rstd2 = sb("rstd2", [R, 1])
        aot = [sb(f"aot{k}", [128, R]) for k in range(2)]
        xps = sb("xps", [R, D])
        xmt = [sb(f"xmt{k}", [128, R]) for k in range(2)]
        lg = sb("lg", [R, 2 * E])
        top8 = sb("top8", [R, 8])
        top2 = sb("top2", [R, 8])
        lrep = sb("lrep", [R, 2 * E])
        sel = sb("sel", [R, E])
        lsh = sb("lsh", [R, E])
        pe8 = sb("pe8", [R, E])
        psel = sb("psel", [R, E])
        psum1 = sb("psum1", [R, 1])
        pinv1 = sb("pinv1", [R, 1])
        cmb = sb("cmb", [R, E])
        cmbt = sb("cmbt", [E, R])
        xm_end = sb("xm_end", [128, T * R], F32R)
        hf = [sb(f"hf{k}", [128, NB * R]) for k in range(2)]
        w1t = [[sb(f"w1t{p}{k}", [128, DFF]) for k in range(2)] for p in range(2)]
        w2t = [sb(f"w2t{p}", [128, FC, D]) for p in range(2)]

        gall = sb("gall", [R, GROUPS, R], stack=early)
        X = [sb(f"x_{s}", [R, HC, R], stack=early) for s in range(CH)]
        P = [sb(f"p_{s}", [R, HC, R], stack=early) for s in range(CH)]
        Y = [sb(f"y_{s}", [R, HC, R], stack=early) for s in range(CH)]
        W = [sb(f"w_{s}", [R, HC, R], stack=early) for s in range(CH)]
        early.close()
        w1_hi = [[sb(f"w1_hi{p}{k}", [128, DFF], F32R) for k in range(2)] for p in range(2)]
        w1_lo = [[sb(f"w1_lo{p}{k}", [(128, KB)[k], DFF], F32R) for k in range(2)] for p in range(2)]
        w2_hl = [sb(f"w2_hl{p}", [128, FC, 2 * D], F32R) for p in range(2)]
        h_hi = [sb(f"h_hi{k}", [128, FC, NB * R], F32R) for k in range(2)]
        h_lo = [sb(f"h_lo{k}", [128, FC, NB * R], F32R) for k in range(2)]

        bank = [psum(f"bank{i}", [128, 512]) for i in range(8)]
        scp, btp, gp, avp, f0, f1 = bank[0:3], bank[3], bank[4], bank[5], bank[6], bank[7]
        inv_bank, f = bank[0:3], bank[3:8]
        h_bank, y_bank = [*bank[0:3], f1], [*bank[3:6], f0]

        first_in = sem("first_in")
        consts_in = sem("consts_in")
        weights_in = sem("weights_in")
        patches_in = sem("patches_in")
        out_done = sem("out_done")
        fixed = sem("fixed")
        bias_ps = sem("bias_ps")
        post_done = sem("post_done")

        lin_ps, var_done, rstd_done, norm_done = sem("lin_ps"), sem("var_done"), sem("rstd_done"), sem("norm_done")
        xt_ps, xt_sb, q_ps, k_ps, v_ps = sem("xt_ps"), sem("xt_sb"), sem("q_ps"), sem("k_ps"), sem("v_ps")
        q_sb, k_sb, v_sb = sem("q_sb"), sem("k_sb"), sem("v_sb")
        prt_ps, prt_sb, av_sb = sem("prt_ps"), sem("prt_sb"), sem("av_sb")
        dve_step, pool_step = sem("dve_step"), sem("pool_step")
        sc_ps, g_ps = sems("sc_ps", CH), sems("g_ps", CH)
        zr_done = sems("zr_done", CH)
        sub_done, exp_done, pr_done = sems("sub_done", CH), sems("exp_done", CH), sems("pr_done", CH)
        cs_added, cs_half, cs_used = sem("cs_added"), sem("cs_half"), sem("cs_used")
        red_done, redall_done, cinv_step = sem("red_done"), sem("redall_done"), sem("cinv_step")
        x_done, x74_done, y_done = sems("x_done", CH), sems("x74_done", CH), sems("y_done", CH)
        p_done, w_done, half_ps = sems("p_done", CH), sems("w_done", CH), sems("half_ps", CH)
        n_ps, nos_sb = sem("n_ps"), sem("nos_sb")
        a_not_ps, a_not_sb, a_proj_ps = sem("a_not_ps"), sem("a_not_sb"), sem("a_proj_ps")
        a_var, a_rstd, a_pool, a_step = sem("a_var"), sem("a_rstd"), sem("a_pool"), sem("a_step")
        a_norm, a_xt_ps, a_xt_sb = sem("a_norm"), sem("a_xt_ps"), sem("a_xt_sb")
        a_q_ps, a_k_ps, a_v_ps = sem("a_q_ps"), sem("a_k_ps"), sem("a_v_ps")
        a_q_sb, a_k_sb, a_v_sb = sem("a_q_sb"), sem("a_k_sb"), sem("a_v_sb")
        a_sc_ps, a_sub, a_exp, a_prt_ps, a_prt_sb = sem("a_sc_ps"), sem("a_sub"), sem("a_exp"), sem("a_prt_ps"), sem("a_prt_sb")
        b_av_ps, b_ao, b_aot_ps, b_aot_sb, b_mix_ps = sem("b_av_ps"), sem("b_ao"), sem("b_aot_ps"), sem("b_aot_sb"), sem("b_mix_ps")
        b_xp, b_acc, b_var, b_rstd, b_pool, b_step = sem("b_xp"), sem("b_acc"), sem("b_var"), sem("b_rstd"), sem("b_pool"), sem("b_step")
        b_norm, b_xmt_ps, b_xmt_sb, b_xmall = sem("b_norm"), sem("b_xmt_ps"), sem("b_xmt_sb"), sem("b_xmall")
        b_router_ps, b_lg, b_lsh, b_pe8 = sem("b_router_ps"), sem("b_lg"), sem("b_lsh"), sem("b_pe8")
        c_step = sem("c_step")
        c_cmb, c_cmbt_ps, c_cmbt_sb, c_b2_ps, c_b2 = sem("c_cmb"), sem("c_cmbt_ps"), sem("c_cmbt_sb"), sem("c_b2_ps"), sem("c_b2")
        expert_in = sems("expert_in", 2)
        h_ps = sem("h_ps")
        gelu_done = sems("gelu_done", 4)
        high_done = sem("high_done")
        low_done = sem("low_done")
        w1_split, w2_split = sems("w1_split", 2), sems("w2_split", 2)
        acc_low = sem("acc_low")
        y_ps = sems("y_ps", 2)
        y_used = sems("y_used", 4)

        BLOCKS = [(0, 3), (3, 3), (6, 3), (9, 2)]
        BLOCK_ROWS = [sum(ROWS[t0:t0 + nt]) for t0, nt in BLOCKS]
        Y_USES = [len([j for j in range(T) if j % 4 == b]) for b in range(4)]
        Y_TILES = [[j for k in (b, b + 2) for j in range(BLOCKS[k][0], sum(BLOCKS[k]))] for b in range(2)]

        OUT_TILES = [(0, 6), (6, 9), (9, 10), (10, T)]
        W1_SPLITS, W2_SPLITS, XM_SPLITS = 4, 2, 4

        primed = [prt_sb, av_sb, v_sb, k_sb, *sub_done, *exp_done, *g_ps, *x_done, *half_ps,
                  low_done, cs_added, *gelu_done, *y_ps, *y_used]

        def at(semaphore, count):
            count = count + 1 if any(semaphore is x for x in primed) else count
            return max(count, 0) if isinstance(count, int) else count

        def gate(eng):
            eng.nop(nofuse=True)

        block = ctx.enter_context(nc.Block())

        def heads(b, n, m=HC):
            return b[0:R, 0:m * n].rearrange("p (j n) -> p j n", n=n)

        def rounds(eng, one):
            for g in range(3):
                one(g, True, g >= 1, g >= 2, False)
            with eng.Fori(3, T - 1) as g:
                one(g, True, True, True, True)
            one(T - 1, True, True, True, True)
            for g in range(T, T + 3):
                one(g, False, g < T + 1, g < T + 2, True)

        def passes(eng, one):
            one(-2, False, False, True)
            one(-1, False, True, True)
            with eng.Fori(0, T - 2) as t:
                one(t, True, True, True)
            one(T - 2, True, True, False)
            one(T - 1, True, False, False)

        early_units = {}

        def place_units(kind, first, end, g, k0, k1):
            for n in range(first, end):
                early_units.setdefault((g, k0 + (n - first) * (k1 - k0) // (end - first)), []).append((kind, n))

        place_units("hidden", 0, 12, T, 0, 6)
        place_units("down", 0, 3, T, 6, 12)
        place_units("hidden", 12, 18, T + 1, 1, 7)
        place_units("down", 3, 8, T + 1, 7, 12)
        place_units("down", 8, 9, T + 2, 0, 1)
        place_units("hidden", 18, 24, T + 2, 0, 3)
        place_units("down", 9, 11, T + 2, 3, 4)

        def early_y_bank(t):
            return bank[2] if t < NB or t % 2 else bank[5]

        def experts(eng, expert):
            with eng.Fori(0, E // 2 - 1) as i:
                expert(2 * i + 1, 1, i)
                expert(2 * i + 2, 0, i + 1)
            expert(E - 1, 1, E // 2 - 1)

        def block_order(hidden, down):
            for blk in range(len(BLOCKS)):
                hidden(blk)
                if blk:
                    down(blk - 1)
            down(len(BLOCKS) - 1)

        class Chain:

            def __init__(self, eng, sem_):
                self.eng, self.sem, self.base, self.n = eng, sem_, 0, 0

            def done(self, ins):
                self.n += 1
                ins.then_inc(self.sem, 1)

            def wait(self):
                self.eng.wait_ge(self.sem, at(self.sem, self.base + self.n))

        @block.sync
        def _(sp):
            sp.dma_start(btok[:, :], b_tok).then_inc(first_in, 16)
            sp.dma_start(rmask[:, :], row_mask).then_inc(first_in, 16)
            sp.dma_start(pt[:, :], patches[:, 0, :]).then_inc(patches_in, 16)
            sp.dma_start(wtok[:, :, :], w_tok).then_inc(first_in, 16)
            sp.dma_start(post[:, :], pos).then_inc(first_in, 16)
            sp.dma_start(cst[:, :], consts).then_inc(first_in, 16)
            sp.dma_start(xtb1[KB:AUG, :], aug1).then_inc(consts_in, 16)
            sp.dma_start(xtb2[KB:AUG, :], aug2).then_inc(consts_in, 16)
            for k, (lo, hi) in enumerate([(0, 128), (128, 128 + AUG)]):
                sp.dma_start(wqk[0][k][0:hi - lo, :, :], wqk1[lo:hi, :, :]).then_inc(consts_in, 16)
            for k, (lo, hi) in enumerate([(0, 128), (128, D)]):
                sp.dma_start(wv[0][k][0:hi - lo, :], wv1[lo:hi, :]).then_inc(consts_in, 16)
            with sp.Fori(1, T) as t:
                sp.wait_ge(lin_ps, at(lin_ps, t))
                sp.dma_start(pt[:, :], patches[:, t, :]).then_inc(patches_in, 16)
            for k, (lo, hi) in enumerate([(0, 128), (128, 128 + AUG)]):
                sp.dma_start(wqk[1][k][0:hi - lo, :, :], wqk2[lo:hi, :, :]).then_inc(weights_in, 16)
            for k, (lo, hi) in enumerate([(0, 128), (128, D + 1)]):
                for dst, src in ((wv[1], wv2), (wo[0], wproj1), (wo[1], wproj2), (wr, router)):
                    sp.dma_start(dst[k][0:hi - lo, :], src[lo:hi, :]).then_inc(weights_in, 16)
            sp.dma_start(b2t[:, :], b2).then_inc(weights_in, 16)
            sp.dma_start(aff[:, :], affine).then_inc(weights_in, 16)
            sp.dma_start(b1t[:, :, :], b1).then_inc(weights_in, 16)

            def load_expert(e, p):
                sp.dma_start(w1t[p][0][:, :], w1[e, 0:128, :]).then_inc(expert_in[p], 16)
                for half in range(2):
                    sp.dma_start(w1t[p][1][half * KB:(half + 1) * KB, :], w1[e, 128:D, :]).then_inc(expert_in[p], 16)
                sp.dma_start(w2t[p][:, :, :], w2[e, :, :].rearrange("p (c d) -> p c d", c=FC)).then_inc(expert_in[p], 16)

            for p in range(2):
                load_expert(p, p)
            with sp.Fori(1, E // 2) as i:
                for p in range(2):
                    sp.wait_ge(w1_split[p], at(w1_split[p], W1_SPLITS * i))
                    gate(sp)
                    sp.wait_ge(w2_split[p], at(w2_split[p], W2_SPLITS * i))
                    gate(sp)
                    load_expert(2 * i + p, p)
            for t0, t1 in OUT_TILES:
                sp.wait_ge(y_used[(t1 - 1) % 4], at(y_used[(t1 - 1) % 4], (E - 1) * Y_USES[(t1 - 1) % 4] + (t1 - 1) // 4 + 1))
                if t1 < T:
                    for b in range(NB):
                        dst = out[NB * t0:NB * t1, :, :].rearrange("(t b) i d -> b i t d", b=NB)[b]
                        sp.dma_start(dst, hall[b * S:b * S + TOK, t0:t1, :]).then_inc(out_done, 16)
                else:
                    for b in range(LEFT):
                        sp.dma_start(out[NB * t0 + b, :, :], hall[b * S:b * S + TOK, t0, :]).then_inc(out_done, 16)
            sp.wait_ge(out_done, at(out_done, 16 * (NB * (len(OUT_TILES) - 1) + LEFT)))

        FIRST_IN = 16 * 5
        CONSTS_IN = 16 * 6
        WEIGHTS_IN = 16 * 13
        FIXED = 8

        @block.tensor
        def _(pe):
            mm = nc.tensor.matmul

            def tr(dst, src, n):
                return nc.tensor.transpose(dst, src, ident[0:n, 0:n])

            def to_features(src, b):
                tr(b[:, 0:R], src[:, 0:128], R)
                return tr(b[0:KB, R:2 * R], src[:, 128:D], R)

            def queries_or_keys(q, l, xb, dst):
                w = wqk[l]
                for c in range(CH):
                    mm(dst[:, c * R:(c + 1) * R], w[0][:, q, c * 128:(c + 1) * 128], xta[:, :], start=True, stop=False)
                    last = mm(dst[:, c * R:(c + 1) * R], w[1][0:AUG, q, c * 128:(c + 1) * 128], xb[0:AUG, :],
                              start=False, stop=True)
                return last

            def linear(src, w, k, dst, n=D):
                mm(dst[0:R, 0:n], src[0][:, :], w[0][:, :], start=True, stop=False)
                return mm(dst[0:R, 0:n], src[1][0:k, :], w[1][0:k, :], start=False, stop=True)

            def scores(c, dst):
                return mm(dst[0:R, 0:HC * R], qt[:, c * R:(c + 1) * R], ktm[:, c, :, :].rearrange("p j n -> p (j n)"),
                          start=True, stop=True)

            pe.wait_ge(first_in, at(first_in, FIRST_IN))
            mm(f0[0:R, 0:D], rmask[0:1, :], btok[0:1, :], start=True, stop=True).then_inc(bias_ps, 1)

            def embed(t):
                pe.wait_ge(patches_in, at(patches_in, 16 * (t + 1)))
                for k in range(PC):
                    last = mm(f1[0:R, 0:D], pt[:, k * R:(k + 1) * R], wtok[:, k, :], start=(k == 0), stop=(k == PC - 1))
                last.then_inc(lin_ps, 1)

            def hidden_to_features(t):
                pe.wait_ge(norm_done, at(norm_done, t + 1))
                to_features(nrm, f1).then_inc(xt_ps, 1)

            def keys1(t):
                if isinstance(t, int) and t == 0:
                    pe.wait_ge(consts_in, at(consts_in, CONSTS_IN))
                pe.wait_ge(xt_sb, at(xt_sb, 2 * (t + 1)))
                pe.wait_ge(sub_done[1], at(sub_done[1], t))
                queries_or_keys(1, 0, xtb1, scp[1]).then_inc(k_ps, 1)

            def queries1(t):
                pe.wait_ge(sub_done[2], at(sub_done[2], t))
                queries_or_keys(0, 0, xtb1, scp[2]).then_inc(q_ps, 1)

            def values1(t):
                pe.wait_ge(v_sb, at(v_sb, t))
                linear([xta, xtb1], wv[0], KB, f0).then_inc(v_ps, 1)

            def scores1(t, c):
                if c == 0:
                    pe.wait_ge(q_sb, at(q_sb, t + 1))
                    pe.wait_ge(k_sb, at(k_sb, HC * (t + 1)))
                    pe.wait_ge(sub_done[0], at(sub_done[0], t))
                scores(c, scp[c]).then_inc(sc_ps[c], 1)

            def transpose1(t, c):
                pe.wait_ge(pr_done[c], at(pr_done[c], t + 1))
                pe.wait_ge(prt_sb, at(prt_sb, CH * t + c))
                for j in range(HC):
                    last = tr(btp[0:R, j * R:(j + 1) * R], pr[:, c, j, :], R)
                last.then_inc(prt_ps, 1)

            def gram(t, c):
                pe.wait_ge(prt_sb, at(prt_sb, CH * t + c + 1))
                pe.wait_ge(av_sb, at(av_sb, CH * t + c))
                if c == 0:
                    pe.wait_ge(v_sb, at(v_sb, t + 1))
                n = R + DH + 1
                for j in range(HC):
                    b = (gp, avp)[j // 2]
                    last = mm(b[0:R, j % 2 * n:(j % 2 + 1) * n], prt[:, c, j, 0:R], prt[:, c, j, :], start=True, stop=True)
                last.then_inc(g_ps[c], 1)

            def one(t, tile, middle, front):
                if front:
                    embed(t + 2)
                if middle:
                    values1(t + 1)
                    scores1(t + 1, 0)
                if tile:
                    transpose1(t, 0)
                if middle:
                    scores1(t + 1, 1)
                if tile:
                    transpose1(t, 1)
                    gram(t, 0)
                if front:
                    hidden_to_features(t + 2)
                if middle:
                    scores1(t + 1, 2)
                if tile:
                    transpose1(t, 2)
                    gram(t, 1)
                if front:
                    keys1(t + 2)
                    queries1(t + 2)
                if tile:
                    gram(t, 2)

            pe.wait_ge(post_done, at(post_done, 1))
            passes(pe, one)

            pe.wait_ge(weights_in, at(weights_in, WEIGHTS_IN))

            def half_step(g, k, s):
                n = k // 2
                if k % 2 == 0:
                    pe.wait_ge(x_done[s], at(x_done[s], 7 * g + n + 1))
                    left, right = X[s], X[s]
                else:
                    pe.wait_ge(p_done[s], at(p_done[s], ITERS * g + n + 1))
                    pe.wait_ge(w_done[s], at(w_done[s], ITERS * g + n + 1))
                    left, right = P[s], W[s]
                for j in range(HC):
                    last = mm(inv_bank[s][0:R, j * R:(j + 1) * R], left[:, j, :], right[:, j, :], start=True, stop=True)
                last.then_inc(half_ps[s], 1)

            def apply_inverse(t, s):
                if s == 0:
                    pe.wait_ge(b_xmt_sb, at(b_xmt_sb, 2 * (t - 1)))
                pe.wait_ge(x_done[s], at(x_done[s], 7 * t + 7))
                for h in range(s * HC, (s + 1) * HC):
                    last = mm(f[1][0:R, h * DH:(h + 1) * DH], XF[s][:, h - s * HC, :],
                              avall[:, bass.ds(t * H + h, 1), 0:DH].rearrange("p g n -> p (g n)"), start=True, stop=True)
                if s == CH - 1:
                    last.then_inc(n_ps, 1)

            def transpose2(t, c):
                pe.wait_ge(a_exp, at(a_exp, CH * t + c + 1))
                for j in range(HC):
                    last = tr(f[2][0:R, j * R:(j + 1) * R], pr[:, c, j, :], R)
                last.then_inc(a_prt_ps, 1)

            def attend(t, c):
                pe.wait_ge(a_prt_sb, at(a_prt_sb, CH * t + c + 1))
                for j in range(HC):
                    last = mm(f[3][0:R, j * (DH + 1):(j + 1) * (DH + 1)], prt[:, c, j, 0:R], v1[:, c * HC + j, :],
                              start=True, stop=True)
                last.then_inc(b_av_ps, 1)

            def stage_a(t, k):
                if k == 1:
                    pe.wait_ge(nos_sb, at(nos_sb, t + 1))
                    pe.wait_ge(b_lg, at(b_lg, t - 1))
                    to_features(nos, f[0]).then_inc(a_not_ps, 1)
                if k == 2:
                    pe.wait_ge(a_not_sb, at(a_not_sb, 2 * (t + 1)))
                    linear(aot, wo[0], KB + 1, f[1]).then_inc(a_proj_ps, 1)
                if k == 5:
                    pe.wait_ge(a_norm, at(a_norm, t + 1))
                    to_features(nrm, f[0]).then_inc(a_xt_ps, 1)
                if k == 6:
                    pe.wait_ge(a_xt_sb, at(a_xt_sb, 2 * (t + 1)))
                    pe.wait_ge(a_prt_sb, at(a_prt_sb, CH * t))
                    queries_or_keys(0, 1, xtb2, f[2]).then_inc(a_q_ps, 1)
                    pe.wait_ge(b_ao, at(b_ao, CH * t))
                    queries_or_keys(1, 1, xtb2, f[3]).then_inc(a_k_ps, 1)
                if k == 7:
                    pe.wait_ge(a_q_sb, at(a_q_sb, t + 1))
                    pe.wait_ge(a_k_sb, at(a_k_sb, HC * (t + 1)))
                    scores(0, f[3]).then_inc(a_sc_ps, 1)
                if k == 8:
                    pe.wait_ge(c_b2, at(c_b2, t - 1))
                    scores(1, f[4]).then_inc(a_sc_ps, 1)
                if k == 9:
                    pe.wait_ge(a_sub, at(a_sub, CH * t + 1))
                    scores(2, f[3]).then_inc(a_sc_ps, 1)
                if k == 10:
                    linear([xta, xtb2], wv[1], KB + 1, f[2]).then_inc(a_v_ps, 1)
                if k == 11:
                    pe.wait_ge(a_v_sb, at(a_v_sb, t + 1))
                    transpose2(t, 0)

            def stage_b(t, k):
                if k < 2:
                    pe.wait_ge(a_prt_sb, at(a_prt_sb, CH * t + k + 1))
                    transpose2(t, k + 1)
                if k == 1:
                    pe.wait_ge(a_sub, at(a_sub, CH * t + CH))
                    attend(t, 0)
                if k in (2, 3):
                    pe.wait_ge(b_ao, at(b_ao, CH * t + k - 1))
                    attend(t, k - 1)
                if k == 5:
                    pe.wait_ge(b_ao, at(b_ao, CH * (t + 1)))
                    to_features(aos, f[1]).then_inc(b_aot_ps, 1)
                if k == 6:
                    pe.wait_ge(b_aot_sb, at(b_aot_sb, 2 * (t + 1)))
                    linear(aot, wo[1], KB + 1, f[0]).then_inc(b_mix_ps, 1)
                if k == 9:
                    pe.wait_ge(b_norm, at(b_norm, t + 1))
                    to_features(nrm2, f[1]).then_inc(b_xmt_ps, 1)
                if k == 10:
                    pe.wait_ge(b_xmt_sb, at(b_xmt_sb, 2 * (t + 1)))
                    linear(xmt, wr, KB + 1, f[0], E).then_inc(b_router_ps, 1)

            def stage_c(t, k):
                if k == 1:
                    pe.wait_ge(c_cmb, at(c_cmb, t + 1))
                    pe.wait_ge(a_sub, at(a_sub, min(CH * (t + 1) + 2, CH * T) if isinstance(t, int) else CH * (t + 1) + 2))
                    tr(f[4][0:E, 0:R], cmb[:, :], R).then_inc(c_cmbt_ps, 1)
                if k == 2:
                    pe.wait_ge(c_cmbt_sb, at(c_cmbt_sb, t + 1))
                    mm(f[4][0:R, 0:D], cmbt[:, :], b2t[:, :], start=True, stop=True).then_inc(c_b2_ps, 1)

            def one(g, inverse, a, b, c):
                for k in range(SLOTS):
                    for s in range(CH):
                        if inverse:
                            half_step(g, k, s)
                        if a and k == 0:
                            apply_inverse(g - 1, s)
                    if a:
                        stage_a(g - 1, k)
                    if b:
                        stage_b(g - 2, k)
                    if c:
                        stage_c(g - 3, k)
                    for unit in early_units.get((g, k), []) if not inverse else []:
                        early(*unit)

            def hidden_chunk(e, p, i, b):
                blk, f = i // FC, i % FC
                t0, n = BLOCKS[blk][0], BLOCK_ROWS[blk]
                cols = slice(t0 * R, t0 * R + n)
                dst = b[:, 0:n]
                w = slice(f * 128, (f + 1) * 128)
                mm(dst, w1_lo[p][1][:, w], xm_end[0:KB, cols], start=True, stop=False)
                mm(dst, w1_lo[p][0][:, w], xm_hi[:, cols], start=False, stop=False)
                mm(dst, w1_hi[p][0][:, w], xm_lo[:, cols], start=False, stop=False)
                mm(dst, w1_hi[p][1][:, w], xm_end[:, cols], start=False, stop=False)
                mm(dst, w1_hi[p][0][:, w], xm_hi[:, cols], start=False, stop=True).then_inc(h_ps, 1)

            def down_tile(e, p, t, b):
                blk = min(t // NB, len(BLOCKS) - 1)
                t0 = BLOCKS[blk][0]
                m = ROWS[t]
                rows = slice((t - t0) * R, (t - t0) * R + m)
                for f in range(FC):
                    if t == t0:
                        pe.wait_ge(low_done, at(low_done, e * FC * 4 + blk * FC + f + 1))
                    mm(b[0:m, 0:2 * D], h_hi[blk % 2][:, f, rows], w2_hl[p][:, f, :], start=(f == 0), stop=False)
                    last = mm(b[0:m, 0:D], h_lo[blk % 2][:, f, rows], w2_hl[p][:, f, 0:D], start=False, stop=(f == FC - 1))
                last.then_inc(y_ps[blk % 2], 1)

            def early(kind, n):
                if kind == "hidden":
                    if n % FC == 0:
                        pe.wait_ge(b_xmall, at(b_xmall, XM_SPLITS * sum(BLOCKS[n // FC])))
                    if n == 0:
                        pe.wait_ge(w1_split[0], at(w1_split[0], W1_SPLITS))
                    if n >= 2:
                        pe.wait_ge(gelu_done[(n - 2) % 4], at(gelu_done[(n - 2) % 4], (n - 2) // 4 + 1))
                    hidden_chunk(0, 0, n, bank[n % 2])
                else:
                    if n == 0:
                        pe.wait_ge(w2_split[0], at(w2_split[0], W2_SPLITS))
                    before = n - (1 if n <= NB else 2)
                    if before >= 0:
                        pe.wait_ge(y_used[before % 4], at(y_used[before % 4], before // 4 + 1))
                    down_tile(0, 0, n, early_y_bank(n))

            rounds(pe, one)

            pe.wait_ge(c_b2, at(c_b2, T))
            for n in range(4 * FC - 2, 4 * FC):
                pe.wait_ge(gelu_done[n % 4], at(gelu_done[n % 4], n // 4 + 1))
            for t in range(T - 2, T):
                pe.wait_ge(y_used[t % 4], at(y_used[t % 4], t // 4 + 1))

            def expert(e, p, n):
                def hidden(blk):
                    for i in range(blk * FC, (blk + 1) * FC):
                        pe.wait_ge(gelu_done[i % 4], at(gelu_done[i % 4], e * FC + i // 4))
                        hidden_chunk(e, p, i, h_bank[i % 4])

                def down(blk):
                    if blk == 0:
                        pe.wait_ge(w2_split[p], at(w2_split[p], W2_SPLITS * (n + 1)))
                    for t in range(BLOCKS[blk][0], sum(BLOCKS[blk])):
                        pe.wait_ge(y_used[t % 4], at(y_used[t % 4], e * Y_USES[t % 4] + t // 4))
                        down_tile(e, p, t, y_bank[t % 4])

                pe.wait_ge(w1_split[p], at(w1_split[p], W1_SPLITS * (n + 1)))
                block_order(hidden, down)

            experts(pe, expert)

        @block.scalar
        def _(act):
            def copy(dst, src):
                return nc.scalar.activation(dst, src, ACT.Copy)

            def affine_out(dst, src, k, which):
                n = 128 if k == 0 else KB
                c = 4 * k + 2 * which
                return nc.scalar.activation(dst, src, ACT.Identity, bias=aff[0:n, c + 1:c + 2], scale=aff[0:n, c:c + 1])

            def keys_out(src, done, heads_here=2):
                for j in range(heads_here):
                    q = slice(32 * j, 32 * j + 32)
                    copy(ktm[q, :, j, :], src[q, 0:CH * R].rearrange("p (c n) -> p c n", n=R)).then_inc(done, 1)

            def by_head(ap):
                return ap.rearrange("p (h d) -> p h d", d=DH)

            def xt_out(t):
                act.wait_ge(xt_ps, at(xt_ps, t + 1))
                copy(xta[:, :], f1[:, 0:R]).then_inc(xt_sb, 1)
                copy(xtb1[0:KB, :], f1[0:KB, R:2 * R]).then_inc(xt_sb, 1)

            def qk_out(t):
                act.wait_ge(k_ps, at(k_ps, t + 1))
                act.wait_ge(fixed, at(fixed, FIXED))
                keys_out(scp[1], k_sb, HC)
                act.wait_ge(q_ps, at(q_ps, t + 1))
                copy(qt[:, :], scp[2][:, 0:CH * R]).then_inc(q_sb, 1)

            def v_out(t):
                act.wait_ge(v_ps, at(v_ps, t + 1))
                act.wait_ge(g_ps[2], at(g_ps[2], t))
                copy(prt[:, :, :, R:R + DH].rearrange("p c j d -> p (c j) d"), by_head(f0[0:R, 0:D])).then_inc(v_sb, 1)

            def exp1(t, c):
                act.wait_ge(sub_done[c], at(sub_done[c], t + 1))
                nc.scalar.activation(pr[:, c], sd[:, c], ACT.Exp, scale=DH ** -0.5).then_inc(exp_done[c], 1)

            def prt_out(t, c):
                act.wait_ge(prt_ps, at(prt_ps, CH * t + c + 1))
                if c == 0:
                    act.wait_ge(cs_added, at(cs_added, t))
                gate(act)
                src = heads(btp, R)
                copy(prt[:, c, :, 0:R], src).then_inc(prt_sb, 1)

            def gram_out(t, c):
                act.wait_ge(g_ps[c], at(g_ps[c], t + 1))
                gate(act)
                for i, b in enumerate((gp, avp)):
                    src = heads(b, R + DH + 1, 2)
                    copy(gall[:, bass.ds(t * H + (c * HC + 2 * i), 2), :], src[:, :, 0:R])
                    last = copy(avall[:, bass.ds(t * H + (c * HC + 2 * i), 2), 0:DH + 1], src[:, :, R:R + DH + 1])
                last.then_inc(av_sb, 1)

            def one(t, tile, middle, front):
                if tile:
                    prt_out(t, 0)
                if middle:
                    exp1(t + 1, 0)
                if tile:
                    prt_out(t, 1)
                    gram_out(t, 0)
                if front:
                    xt_out(t + 2)
                if middle:
                    exp1(t + 1, 1)
                if tile:
                    prt_out(t, 2)
                if middle:
                    exp1(t + 1, 2)
                if tile:
                    gram_out(t, 1)
                if front:
                    qk_out(t + 2)
                if tile:
                    gram_out(t, 2)
                if middle:
                    v_out(t + 1)

            passes(act, one)

            act.wait_ge(weights_in, at(weights_in, WEIGHTS_IN))

            def x74(s, count):
                act.wait_ge(x_done[s], at(x_done[s], count))
                nc.scalar.activation(Y[s][:, :, :], X[s][:, :, :], ACT.Copy, scale=1.75).then_inc(x74_done[s], 1)

            def half_step(g, k):
                n = k // 2
                for s in range(CH):
                    if k % 2 == 0:
                        act.wait_ge(half_ps[s], at(half_ps[s], SLOTS * g + k + 1))
                        copy(P[s][:, :, :], heads(inv_bank[s], R)).then_inc(p_done[s], 1)
                    elif n < ITERS - 1:
                        x74(s, 7 * g + n + 2)

            def features_out(dst, src, done):
                copy(dst[0][:, :], src[:, 0:R]).then_inc(done, 1)
                copy(dst[1][0:KB, :], src[0:KB, R:2 * R]).then_inc(done, 1)

            def affine_out2(dst, src, done, which):
                affine_out(dst[0][:, :], src[:, 0:R], 0, which).then_inc(done, 1)
                affine_out(dst[1][0:KB, :], src[0:KB, R:2 * R], 1, which).then_inc(done, 1)

            def transpose_out(t, c):
                act.wait_ge(a_prt_ps, at(a_prt_ps, CH * t + c + 1))
                copy(prt[:, c, :, 0:R], heads(f[2], R)).then_inc(a_prt_sb, 1)

            def stage_a(t, k):
                if k == 0:
                    act.wait_ge(n_ps, at(n_ps, t + 1))
                    copy(nos[:, :], f[1][0:R, 0:D]).then_inc(nos_sb, 1)
                if k == 1:
                    act.wait_ge(a_not_ps, at(a_not_ps, t + 1))
                    features_out(aot, f[0], a_not_sb)
                if k == 5:
                    act.wait_ge(a_xt_ps, at(a_xt_ps, t + 1))
                    affine_out2([xta, xtb2], f[0], a_xt_sb, 0)
                if k == 6:
                    act.wait_ge(a_q_ps, at(a_q_ps, t + 1))
                    copy(qt[:, :], f[2][:, 0:CH * R]).then_inc(a_q_sb, 1)
                    act.wait_ge(a_k_ps, at(a_k_ps, t + 1))
                    keys_out(f[3], a_k_sb)
                if k == 10:
                    act.wait_ge(a_v_ps, at(a_v_ps, t + 1))
                    copy(v1[:, :, 0:DH], by_head(f[2][0:R, 0:D])).then_inc(a_v_sb, 1)
                if k in (8, 9, 10):
                    c = k - 8
                    act.wait_ge(a_sub, at(a_sub, CH * t + c + 1))
                    nc.scalar.activation(pr[:, c], sd[:, c], ACT.Exp, scale=DH ** -0.5).then_inc(a_exp, 1)
                if k == 11:
                    transpose_out(t, 0)

            def stage_b(t, k):
                if k < 2:
                    transpose_out(t, k + 1)
                if k == 5:
                    act.wait_ge(b_aot_ps, at(b_aot_ps, t + 1))
                    features_out(aot, f[1], b_aot_sb)
                if k == 9:
                    act.wait_ge(b_xmt_ps, at(b_xmt_ps, t + 1))
                    act.wait_ge(b_xmall, at(b_xmall, XM_SPLITS * t))
                    affine_out2(xmt, f[1], b_xmt_sb, 1)

            def stage_c(t, k):
                if k == 0:
                    act.wait_ge(b_lsh, at(b_lsh, t + 1))
                    nc.scalar.activation(pe8[:, :], lsh[:, :], ACT.Exp).then_inc(b_pe8, 1)
                if k == 1:
                    act.wait_ge(c_cmbt_ps, at(c_cmbt_ps, t + 1))
                    copy(cmbt[:, :], f[4][0:E, 0:R]).then_inc(c_cmbt_sb, 1)

            def one(g, inverse, a, b, c):
                if inverse:
                    for s in range(CH):
                        x74(s, 7 * g + 1)
                for k in range(SLOTS):
                    if inverse:
                        half_step(g, k)
                    if a:
                        stage_a(g - 1, k)
                    if b:
                        stage_b(g - 2, k)
                    if c:
                        stage_c(g - 3, k)
                    for unit in early_units.get((g, k), []) if not inverse else []:
                        early(*unit)

            def gelu_chunk(e, i, b):
                blk, f = i // FC, i % FC
                n = BLOCK_ROWS[blk]
                act.wait_ge(h_ps, at(h_ps, e * FC * 4 + i + 1))
                if f == 0:
                    act.wait_ge(y_ps[blk % 2], at(y_ps[blk % 2], e * len(Y_TILES[blk % 2]) + (3 if blk > 1 else 0)))
                gate(act)
                nc.scalar.activation(h_hi[blk % 2][:, f, 0:n], b[:, 0:n], ACT.Gelu,
                                     bias=b1t[:, e, f:f + 1]).then_inc(high_done, 1)
                act.wait_ge(low_done, at(low_done, e * FC * 4 + max(i - 1, 0)))
                gate(act)
                nc.scalar.activation(hf[i % 2][:, 0:n], b[:, 0:n], ACT.Gelu,
                                     bias=b1t[:, e, f:f + 1]).then_inc(gelu_done[i % 4], 1)

            def early(kind, n):
                if kind == "hidden":
                    gelu_chunk(0, n, bank[n % 2])

            rounds(act, one)

            def expert(e, p, n):
                for i in range(4 * FC):
                    gelu_chunk(e, i, h_bank[i % 4])

            experts(act, expert)

        @block.vector
        def _(dve):
            V = nc.vector

            def norm_stats(ch, st, m, src, var_sem):
                ch.wait()
                gate(dve)
                ch.done(V.bn_stats(st[:, :], src))
                ch.wait()
                gate(dve)
                V.bn_aggr(m[:, :], st[:, :]).then_inc(var_sem, 1)

            def wide(ap):
                return ap.unsqueeze(2).to_broadcast([R, HC, R])

            def shift(ch, c, src, done):
                ch.done(V.tensor_reduce(mx[:, c, :], heads(src, R), axis=AX.X, op=ALU.max))
                ch.wait()
                V.tensor_tensor(sd[:, c], heads(src, R), wide(mx[:, c, :]), ALU.subtract).then_inc(done, 1)

            def keys_out(src, done):
                for j in range(2, HC):
                    q = slice(32 * j, 32 * j + 32)
                    V.tensor_copy(ktm[q, :, j, :], src[q, 0:CH * R].rearrange("p (c n) -> p c n", n=R)).then_inc(done, 1)

            V.memset(ktm[:, :, :, :], 0.0).then_inc(fixed, 1)
            V.memset(v1[:, :, DH:DH + 1], 1.0).then_inc(fixed, 1)
            V.memset(aot[1][KB:KB + 1, :], 1.0).then_inc(fixed, 1)
            V.memset(xmt[1][KB:KB + 1, :], 1.0).then_inc(fixed, 1)
            V.memset(lg[:, E:2 * E], -3.0e38).then_inc(fixed, 1)
            V.memset(csb[:, :, :], 0.0).then_inc(fixed, 1)
            V.memset(csmax[:, :], 0.0).then_inc(fixed, 1)
            dve.wait_ge(first_in, at(first_in, FIRST_IN))
            V.tensor_copy(prt[:, :, :, R + DH].rearrange("p c j -> p (c j)"), wcol.to_broadcast([R, H])).then_inc(fixed, 1)
            dve.wait_ge(fixed, at(fixed, FIXED))
            dve.wait_ge(bias_ps, at(bias_ps, 1))
            V.tensor_tensor(post[:, :], post[:, :], f0[0:R, 0:D], ALU.add).then_inc(post_done, 1)
            dve.wait_ge(post_done, at(post_done, 1))

            c1 = Chain(dve, dve_step)

            def front1_a(t):
                dve.wait_ge(lin_ps, at(lin_ps, t + 1))
                c1.done(V.tensor_tensor(hall[:, t, :], f1[0:R, 0:D], post[:, :], ALU.add))
                norm_stats(c1, stats, mv, hall[:, t, :], var_done)

            def front1_b(t):
                dve.wait_ge(rstd_done, at(rstd_done, t + 1))
                V.tensor_scalar(nrm[:, :], hall[:, t, :], mv[:, 0:1], rstd[:, :], ALU.subtract, ALU.mult).then_inc(norm_done, 1)

            def shift1(t, c):
                dve.wait_ge(sc_ps[c], at(sc_ps[c], t + 1))
                dve.wait_ge(exp_done[c], at(exp_done[c], t))
                shift(c1, c, scp[c], sub_done[c])

            def softmax_norm(t, c):
                dve.wait_ge(exp_done[c], at(exp_done[c], t + 1))
                pads = pr[:, c].rearrange("p j (b n) -> p j b n", n=S)[:, :, :, S - 1]
                c1.done(V.tensor_reduce(zs[:, c, :], pr[:, c], axis=AX.X, op=ALU.add))
                c1.done(V.tensor_reduce(zp[:, c, :], pads, axis=AX.X, op=ALU.add))
                c1.wait()
                c1.done(V.scalar_tensor_tensor(zr[:, c, :], zp[:, c, :], float(PADS - 1), zs[:, c, :], ALU.mult, ALU.add))
                c1.done(V.tensor_scalar(pads, pads, ROOT, None, ALU.mult))
                c1.wait()
                c1.done(V.reciprocal(zs[:, c, :], zr[:, c, :]))
                c1.wait()
                V.tensor_scalar(zr[:, c, :], zs[:, c, :], wcol, None, ALU.mult).then_inc(zr_done[c], 1)

            PER_PASS = 2 + CH * (1 + 5) + 2
            BEFORE = {-2: 0}

            def column_sums(tiles):
                if not (isinstance(tiles, int) and tiles == 0):
                    dve.wait_ge(cs_added, at(cs_added, tiles))
                c1.done(V.tensor_reduce(cs[:, :], csb[:, :, :], axis=AX.X, op=ALU.add))
                c1.wait()
                c1.done(V.scalar_tensor_tensor(cs[:, :], csb[:, :, S - 1], ROOT - 1.0, cs[:, :], ALU.mult, ALU.add))
                c1.wait()
                V.tensor_tensor(csmax[:, :], csmax[:, :], cs[:, :], ALU.max).then_inc(cs_used, 1)

            def one(t, tile, middle, front):
                c1.base, c1.n = BEFORE[t] if isinstance(t, int) else BEFORE[0] + t * PER_PASS, 0
                if front:
                    front1_a(t + 2)
                if middle:
                    shift1(t + 1, 0)
                if front:
                    front1_b(t + 2)
                if tile:
                    column_sums(t)
                if middle:
                    shift1(t + 1, 1)
                    softmax_norm(t + 1, 0)
                    shift1(t + 1, 2)
                    softmax_norm(t + 1, 1)
                if middle:
                    softmax_norm(t + 1, 2)
                if isinstance(t, int):
                    BEFORE[t + 1] = c1.base + c1.n
                else:
                    assert c1.n == PER_PASS
                    BEFORE[T - 2] = BEFORE[0] + (T - 2) * PER_PASS

            passes(dve, one)
            c1.base, c1.n = BEFORE[T], 0

            column_sums(T)
            dve.wait_ge(cs_used, at(cs_used, T + 1))
            dve.wait_ge(av_sb, at(av_sb, CH * T))
            c2 = Chain(dve, cinv_step)
            c2.done(V.tensor_reduce(red[:, 0:1], avall[:, :, DH:DH + 1].rearrange("p g n -> p n g"), axis=AX.X, op=ALU.max))
            c2.wait()
            c2.done(V.tensor_reduce(red[:, 1:2], csmax[:, :], axis=AX.X, op=ALU.max))
            c2.wait()
            V.tensor_scalar(red[:, :], red[:, :], winv, None, ALU.mult).then_inc(red_done, 1)
            dve.wait_ge(redall_done, at(redall_done, 1))
            c2.done(V.tensor_tensor(cc[:, :], redall[:, 0:1], redall[:, 1:2], ALU.mult))
            c2.wait()
            c2.done(V.reciprocal(cinv[:, :], cc[:, :]))
            c2.wait()

            ca, cb = Chain(dve, a_step), Chain(dve, b_step)

            def first_x(g, s):
                dve.wait_ge(x_done[s], at(x_done[s], 7 * g))
                V.tensor_scalar(X[s][:, :, :], gall[:, bass.ds(g * H + s * HC, HC), :], cinv[:, :], None, ALU.mult)\
                    .then_inc(x_done[s], 1)

            def half_step(g, k):
                n = k // 2
                for s in range(CH):
                    if k % 2 == 0:
                        dve.wait_ge(p_done[s], at(p_done[s], ITERS * g + n + 1))
                        dve.wait_ge(y_done[s], at(y_done[s], ITERS * g + n + 1))
                        V.scalar_tensor_tensor(W[s][:, :, :], P[s][:, :, :], -0.25, Y[s][:, :, :], ALU.mult, ALU.add)\
                            .then_inc(w_done[s], 1)
                    else:
                        dve.wait_ge(half_ps[s], at(half_ps[s], SLOTS * g + k + 1))
                        new = XF[s] if k == SLOTS - 1 else X[s]
                        V.scalar_tensor_tensor(new[:, :, :], X[s][:, :, :], 3.25, heads(inv_bank[s], R), ALU.mult, ALU.add)\
                            .then_inc(x_done[s], 1)
                        if k == SLOTS - 1 and not (isinstance(g, int) and g == T - 1):
                            first_x(g + 1, s)

            def shift2(t, c, src):
                dve.wait_ge(a_sc_ps, at(a_sc_ps, CH * t + c + 1))
                shift(ca, c, src, a_sub)

            def attention_out(t, c):
                dve.wait_ge(b_av_ps, at(b_av_ps, CH * t + c + 1))
                av = heads(f[3], DH + 1)
                cb.done(V.reciprocal(zs[:, c, :].unsqueeze(2), av[:, :, DH:DH + 1]))
                cb.wait()
                V.tensor_tensor(aos[:, c * HC * DH:(c + 1) * HC * DH].rearrange("p (j d) -> p j d", d=DH),
                                av[:, :, 0:DH], zs[:, c, :].unsqueeze(2).to_broadcast([R, HC, DH]), ALU.mult).then_inc(b_ao, 1)

            def stage_a(t, k):
                if k == 2:
                    dve.wait_ge(a_proj_ps, at(a_proj_ps, t + 1))
                    ca.done(V.tensor_tensor(hall[:, t, :], hall[:, t, :], f[1][0:R, 0:D], ALU.add))
                    norm_stats(ca, stats, mv, hall[:, t, :], a_var)
                if k == 3:
                    dve.wait_ge(a_rstd, at(a_rstd, 2 * t + 1))
                    ca.done(V.tensor_scalar(uall[:, t, :], hall[:, t, :], mv[:, 0:1], rstd[:, :], ALU.subtract, ALU.mult))
                    norm_stats(ca, stats, mv, uall[:, t, :], a_var)
                if k == 4:
                    dve.wait_ge(a_rstd, at(a_rstd, 2 * t + 2))
                    V.tensor_scalar(nrm[:, :], uall[:, t, :], mv[:, 0:1], rstd[:, :], ALU.subtract, ALU.mult).then_inc(a_norm, 1)
                if k == 6:
                    dve.wait_ge(a_k_ps, at(a_k_ps, t + 1))
                    keys_out(f[3], a_k_sb)
                if k == 7:
                    shift2(t, 0, f[3])
                if k == 8:
                    shift2(t, 1, f[4])
                if k == 9:
                    shift2(t, 2, f[3])

            def stage_b(t, k):
                if k in (1, 2, 3):
                    attention_out(t, k - 1)
                if k == 6:
                    dve.wait_ge(b_mix_ps, at(b_mix_ps, t + 1))
                    V.tensor_tensor(xps[:, :], uall[:, t, :], f[0][0:R, 0:D], ALU.add).then_inc(b_xp, 1)
                    dve.wait_ge(b_xp, at(b_xp, t + 1))
                    norm_stats(cb, stats2, mv2, xps[:, :], b_var)
                if k == 8:
                    dve.wait_ge(b_rstd, at(b_rstd, t + 1))
                    V.tensor_scalar(nrm2[:, :], xps[:, :], mv2[:, 0:1], rstd2[:, :], ALU.subtract, ALU.mult).then_inc(b_norm, 1)
            def best_two(t):
                dve.wait_ge(b_router_ps, at(b_router_ps, t + 1))
                V.tensor_copy(lg[:, 0:E], f[0][0:R, 0:E]).then_inc(b_lg, 1)
                dve.wait_ge(b_lg, at(b_lg, t + 1))
                gate(dve)
                cb.done(V.max(top8[:, :], lg[:, 0:E]))
                cb.wait()
                V.tensor_scalar(lsh[:, :], lg[:, 0:E], top8[:, 0:1], None, ALU.subtract).then_inc(b_lsh, 1)
                cb.done(V.tensor_copy(top2[:, 0:2], top8[:, 0:2]))
                cb.done(V.tensor_copy(top2[:, 2:8], lg[:, E:E + 6]))
                cb.wait()
                gate(dve)
                cb.done(V.match_replace(lrep[:, :], top2[:, :], lg[:, :], 3.0e38))
                cb.wait()
                cb.done(V.tensor_tensor(sel[:, :], lrep[:, 0:E], lg[:, 0:E], ALU.not_equal))

            def stage_c(t, k):
                if k == 0:
                    cc3 = Chain(dve, c_step)
                    cc3.base = t * 3
                    dve.wait_ge(b_step, at(b_step, (t + 1) * B_STEPS))
                    dve.wait_ge(b_pe8, at(b_pe8, t + 1))
                    cc3.done(V.tensor_tensor(psel[:, :], pe8[:, :], sel[:, :], ALU.mult))
                    cc3.wait()
                    cc3.done(V.tensor_reduce(psum1[:, :], psel[:, :], axis=AX.X, op=ALU.add))
                    cc3.wait()
                    cc3.done(V.reciprocal(pinv1[:, :], psum1[:, :]))
                    cc3.wait()
                    V.tensor_scalar(cmb[:, :], psel[:, :], pinv1[:, :], None, ALU.mult).then_inc(c_cmb, 1)
                    dve.wait_ge(c_cmb, at(c_cmb, t + 1))
                    V.tensor_copy(comball[:, t, :], cmb[:, :])
                if k == 2:
                    dve.wait_ge(c_b2_ps, at(c_b2_ps, t + 1))
                    dve.wait_ge(b_acc, at(b_acc, t + 1))
                    V.tensor_tensor(hall[:, t, :], hall[:, t, :], f[4][0:R, 0:D], ALU.add).then_inc(c_b2, 1)

            A_STEPS, B_STEPS, BEST_STEPS = 1 + 1 + 1 + 1 + CH, CH + 1 + 5, 5

            def one(g, inverse, a, b, c):
                ca.base, ca.n = (g - 1) * A_STEPS, 0
                if c:
                    cb.base, cb.n = (g - 2) * B_STEPS - BEST_STEPS, 0
                    best_two(g - 3)
                    assert cb.n == BEST_STEPS
                cb.base, cb.n = (g - 2) * B_STEPS, 0
                for k in range(SLOTS):
                    if inverse:
                        half_step(g, k)
                    if a:
                        stage_a(g - 1, k)
                    if b:
                        stage_b(g - 2, k)
                    if c:
                        stage_c(g - 3, k)
                    for unit in early_units.get((g, k), []) if not inverse else []:
                        early(*unit)
                assert not a or ca.n == A_STEPS
                assert not b or cb.n == B_STEPS - BEST_STEPS

            def low_chunk(e, i):
                blk, f = i // FC, i % FC
                n = BLOCK_ROWS[blk]
                dve.wait_ge(gelu_done[i % 4], at(gelu_done[i % 4], e * FC + i // 4 + 1))
                V.tensor_tensor(h_lo[blk % 2][:, f, 0:n], hf[i % 2][:, 0:n], h_hi[blk % 2][:, f, 0:n], ALU.subtract)\
                    .then_inc(low_done, 1)

            def add_tile(e, j, bk):
                m = ROWS[j]
                b = 0 if j in Y_TILES[0] else 1
                dve.wait_ge(y_ps[b], at(y_ps[b], e * len(Y_TILES[b]) + Y_TILES[b].index(j) + 1))
                V.scalar_tensor_tensor(hall[0:m, j, :], bk[0:m, D:2 * D], comball[0:m, j, bass.ds(e, 1)],
                                       hall[0:m, j, :], ALU.mult, ALU.add).then_inc(acc_low, 1)
                dve.wait_ge(acc_low, at(acc_low, e * T + j + 1))
                V.scalar_tensor_tensor(hall[0:m, j, :], bk[0:m, 0:D], comball[0:m, j, bass.ds(e, 1)],
                                       hall[0:m, j, :], ALU.mult, ALU.add).then_inc(y_used[j % 4], 1)

            def early(kind, n):
                if kind == "hidden":
                    low_chunk(0, n)
                else:
                    dve.wait_ge(c_b2, at(c_b2, n + 1))
                    add_tile(0, n, early_y_bank(n))

            for s in range(CH):
                first_x(0, s)
            rounds(dve, one)

            dve.wait_ge(c_b2, at(c_b2, T))

            def expert(e, p, n):
                def hidden(blk):
                    for i in range(blk * FC, (blk + 1) * FC):
                        low_chunk(e, i)

                def down(blk):
                    if blk == 0:
                        for b in range(4):
                            dve.wait_ge(y_used[b], at(y_used[b], e * Y_USES[b]))
                    for j in range(BLOCKS[blk][0], sum(BLOCKS[blk])):
                        add_tile(e, j, y_bank[j % 4])

                block_order(hidden, down)

            experts(dve, expert)

        @block.gpsimd
        def _(pool):
            G = nc.gpsimd
            for x in primed:
                pool.sem_inc(x, 1)
            pool.wait_ge(first_in, at(first_in, FIRST_IN))

            def inv_sqrt(var_sem, m, ve, rs, count, step, done):
                pool.wait_ge(var_sem, at(var_sem, count))
                gate(pool)
                G.tensor_scalar(ve[:, :], m[:, 1:2], EPS, None, ALU.add).then_inc(step, 1)
                pool.wait_ge(step, at(step, count))
                G.tensor_tensor(rs[:, :], ve[:, :], half, ALU.pow).then_inc(done, 1)

            def scale_rows(t, c):
                pool.wait_ge(zr_done[c], at(zr_done[c], t + 1))
                G.tensor_tensor(pr[:, c], pr[:, c], zr[:, c, :].unsqueeze(2).to_broadcast([R, HC, R]), ALU.mult)\
                    .then_inc(pr_done[c], 1)

            def add_blocks(t):
                pool.wait_ge(prt_sb, at(prt_sb, CH * (t + 1)))
                pool.wait_ge(cs_used, at(cs_used, t + 1))
                block = prt[:, :, :, 0:R].rearrange("p c j (b n) -> p (c j) b n", n=S)
                G.tensor_tensor(csb[:, :, :], block[:, :, 0, :], block[:, :, 1, :], ALU.add).then_inc(cs_half, 1)
                pool.wait_ge(cs_half, at(cs_half, t + 1))
                G.tensor_tensor(csb[:, :, :], csb[:, :, :], block[:, :, 2, :], ALU.add).then_inc(cs_added, 1)

            def one(t, tile, middle, front):
                if front:
                    inv_sqrt(var_done, mv, veps, rstd, t + 3, pool_step, rstd_done)
                if middle:
                    scale_rows(t + 1, 0)
                    scale_rows(t + 1, 1)
                if tile:
                    add_blocks(t)
                if middle:
                    scale_rows(t + 1, 2)

            passes(pool, one)

            pool.wait_ge(red_done, at(red_done, 1))
            G.partition_all_reduce(redall[:, :], red[:, :], R, bass.bass_isa.ReduceOp.max).then_inc(redall_done, 1)

            eye = neg_eye.unsqueeze(1).to_broadcast([R, HC, R])

            def finish_y(g, n):
                for s in range(CH):
                    pool.wait_ge(x74_done[s], at(x74_done[s], ITERS * g + n + 1))
                    G.tensor_tensor(Y[s][:, :, :], Y[s][:, :, :], eye, ALU.add).then_inc(y_done[s], 1)

            def stage_a(t, k):
                if k in (2, 3):
                    inv_sqrt(a_var, mv, veps, rstd, 2 * t + k - 1, a_pool, a_rstd)

            def stage_b(t, k):
                if k == 6:
                    inv_sqrt(b_var, mv2, veps2, rstd2, t + 1, b_pool, b_rstd)
                    pool.wait_ge(b_xp, at(b_xp, t + 1))
                    G.tensor_tensor(hall[:, t, :], hall[:, t, :], xps[:, :], ALU.add).then_inc(b_acc, 1)
                if k == 10:
                    pool.wait_ge(b_xmt_sb, at(b_xmt_sb, 2 * (t + 1)))
                    cols = bass.ds(t * R, R)
                    gate(pool)
                    G.tensor_copy(xm_hi[:, cols], xmt[0][:, :]).then_inc(b_xmall, 1)
                    G.tensor_copy(xm_end[0:KB, cols], xmt[1][0:KB, :]).then_inc(b_xmall, 1)
                    pool.wait_ge(b_xmall, at(b_xmall, XM_SPLITS * t + 2))
                    G.tensor_tensor(xm_lo[:, cols], xmt[0][:, :], xm_hi[:, cols], ALU.subtract).then_inc(b_xmall, 1)
                    pool.wait_ge(b_xmall, at(b_xmall, XM_SPLITS * t + 3))
                    G.tensor_tensor(xm_end[KB:2 * KB, cols], xmt[1][0:KB, :], xm_end[0:KB, cols], ALU.subtract).then_inc(b_xmall, 1)
                    pool.wait_ge(b_xmall, at(b_xmall, XM_SPLITS * t + 4))

            def split(p, dst, src, done, count):
                if len(src) == 1:
                    G.tensor_copy(dst, src[0]).then_inc(done[p], 1)
                else:
                    pool.wait_ge(done[p], at(done[p], count))
                    gate(pool)
                    G.tensor_tensor(dst, src[0], src[1], ALU.subtract).then_inc(done[p], 1)

            def split_step(i, p, n):
                if n == 0:
                    pool.wait_ge(expert_in[p], at(expert_in[p], 64 * (i + 1)))
                    gate(pool)
                high2, low2 = w2_hl[p][:, :, 0:D], w2_hl[p][:, :, D:2 * D]
                if n in (0, 1):
                    split(p, w1_hi[p][n][:, :], [w1t[p][n][:, :]], w1_split, None)
                elif n in (2, 3):
                    r = (128, KB)[n - 2]
                    split(p, w1_lo[p][n - 2][:, :], [w1t[p][n - 2][0:r, :], w1_hi[p][n - 2][0:r, :]], w1_split, W1_SPLITS * i + 2)
                elif n == 4:
                    split(p, high2, [w2t[p][:, :, :]], w2_split, None)
                else:
                    split(p, low2, [w2t[p][:, :, :], high2], w2_split, W2_SPLITS * i + 1)

            def one(g, inverse, a, b, c):
                if inverse:
                    finish_y(g, 0)
                for k in range(SLOTS):
                    if inverse and k % 2 == 1 and k < SLOTS - 1:
                        finish_y(g, k // 2 + 1)
                    if a:
                        stage_a(g - 1, k)
                    if b:
                        stage_b(g - 2, k)
                    if inverse and isinstance(g, int) and g == T - 1 and k % 2 == 1:
                        if k == 1:
                            for s in range(CH):
                                pool.wait_ge(x_done[s], at(x_done[s], 7 * g + 1))
                        split_step(0, 0, k // 2)

            rounds(pool, one)
            for n in range(6):
                split_step(0, 1, n)
            with pool.Fori(1, E // 2) as i:
                for p in range(2):
                    for b in range(2):
                        pool.wait_ge(y_ps[b], at(y_ps[b], (2 * i + p - 1) * len(Y_TILES[b])))
                    for n in range(6):
                        split_step(i, p, n)


def kernel(**inputs):
    import concourse.bacc as bacc
    from concourse.bass_utils import run_bass_kernel_spmd

    a = {k: np.asarray(v) for k, v in inputs.items()}
    f = np.float32

    x = a["x"].reshape(IMAGES, GRID, PATCH, GRID, PATCH, 3).transpose(0, 1, 3, 2, 4, 5).reshape(IMAGES, GRID * GRID, PD)
    rows = np.zeros((T, NB, S, PD), f)
    for t in range(T):
        rows[t, :, 1:TOK] = x[TILE_IMAGES[t]]
    patches = rows.reshape(T, R, PC, 128).transpose(3, 0, 2, 1).reshape(128, T, PC * R)
    pos = np.zeros((NB, S, D), f)
    pos[:, 0:TOK] = a["L0_tok_emb_table"][0:TOK]
    w_tok = a["L0_tok_W"].reshape(PC, 128, D).transpose(1, 0, 2)

    consts = np.zeros((128, C_COLS), f)
    consts[:, C_ID:C_ID + 128] = np.eye(128, dtype=f)
    row_mask = np.zeros((1, NB, S), f)
    row_mask[:, :, 1:TOK] = 1
    aug = np.zeros((2, 7, NB, S), f)
    aug[:, 0] = 1
    consts[0:R, C_NEG:C_NEG + R] = -3.75 * np.eye(R, dtype=f)
    for b in range(NB):
        aug[:, 1 + b, b] = 1
        aug[:, 4 + b] = MASK
        aug[:, 4 + b, b] = 0
    aug[1, 4:7, :, S - 1] = MASK
    consts[:, C_W] = consts[:, C_WINV] = 1
    consts[S - 1:R:S, C_W] = ROOT
    consts[S - 1:R:S, C_WINV] = 1 / ROOT
    consts[:, C_HALF] = -0.5

    def qk_layout(w, bias):
        o = np.zeros((128 + AUG, 2, H, 32), f)
        for q in range(2):
            o[0:D, q, :, 0:DH] = w[q * D:(q + 1) * D].T.reshape(D, H, DH)
            if bias is not None:
                o[D, q, :, 0:DH] = bias[q * D:(q + 1) * D].reshape(H, DH)
            for b in range(NB):
                o[D + 1 + NB * q + b, q, :, DH + b] = 1
        return o.reshape(128 + AUG, 2, H * 32)

    def with_bias(w, bias):
        o = np.zeros((w.shape[1] + 1, w.shape[0]), f)
        o[:-1] = w.T
        o[-1] = bias
        return o

    wq, wi = a["L0_attn_w_qkv"], a["L0_ffn_in_proj_w"]
    bi = a["L0_ffn_in_proj_b"]
    affine = np.zeros((128, 8), f)
    for n, name in enumerate(("ln1_g", "ln1_b", "ln2_g", "ln2_b")):
        v = a["L0_ffn_" + name]
        affine[:, n] = v[0:128]
        affine[0:KB, 4 + n] = v[128:D]
    arrays = {
        "patches": patches, "pos": pos.reshape(R, D), "consts": consts,
        "aug1": aug[0].reshape(7, R), "aug2": aug[1].reshape(7, R),
        "w_tok": w_tok, "b_tok": a["L0_tok_b"].reshape(1, D), "row_mask": row_mask.reshape(1, R),
        "wqk1": qk_layout(wq, None), "wv1": wq[2 * D:].T, "wproj1": with_bias(a["L0_attn_w_proj"], a["L0_attn_b_proj"]),
        "wqk2": qk_layout(wi, bi), "wv2": with_bias(wi[2 * D:], bi[2 * D:]),
        "wproj2": with_bias(a["L0_ffn_out_proj_w"], a["L0_ffn_out_proj_b"]),
        "router": with_bias(a["L0_ffn_router_w"], a["L0_ffn_router_b"]),
        "w1": a["L0_ffn_w1"], "b1": a["L0_ffn_b1"].reshape(E, FC, 128).transpose(2, 0, 1),
        "w2": a["L0_ffn_w2"].reshape(E, FC, 128, D).transpose(0, 2, 1, 3).reshape(E, 128, FC * D),
        "b2": a["L0_ffn_b2"], "affine": affine,
    }
    arrays = {k: np.ascontiguousarray(v) for k, v in arrays.items()}
    nc = bacc.Bacc("TRN2", target_bir_lowering=False, num_devices=1)
    aps = {k: nc.dram_tensor(k, v.shape, F32, kind="ExternalInput").ap() for k, v in arrays.items()}
    out = nc.dram_tensor("out", (IMAGES, TOK, D), F32, kind="ExternalOutput").ap()
    build(nc, out=out, **aps)
    r = run_bass_kernel_spmd(nc, [arrays], core_ids=[0])
    return r.results[0]["out"]
```
